# Optimizing a Trainium2 kernel written in Bass

```python
import numpy as np
import jax
import jax.numpy as jnp

def _softmax(x, axis=-1):
    return jax.nn.softmax(x, axis=axis)

def _gelu(x):
    return jax.nn.gelu(x, approximate=True)

def _silu(x):
    return jax.nn.silu(x)

def _sigmoid(x):
    return jax.nn.sigmoid(x)

def _layernorm(x, axis=-1, eps=1e-05):
    m = jnp.mean(x, axis=axis, keepdims=True)
    v = jnp.var(x, axis=axis, keepdims=True)
    return (x - m) / jnp.sqrt(v + eps)

def _scatter_add(tgt, idx, src, axis=0):
    return tgt.at[idx].add(src)

def _segment_sum(src, seg, n):
    return jax.ops.segment_sum(src, seg, n)
kernel_name = 'mk_gnn_resnorm_d2_gnn_r8_6c7c44'

def setup_inputs(seed: int=0):
    np.random.seed(seed)
    _w = jnp.asarray

    def _rec_inputs():
        import jax
        import jax.numpy as jnp
        _gk = jax.random.key(seed)
        x = -0.0005121 + 1.001 * jax.random.normal(jax.random.fold_in(_gk, 1), (12500, 64), jnp.float32)
        src = jax.random.randint(jax.random.fold_in(_gk, 2), (200000,), 0, 12500, jnp.int32)
        dst = jax.random.randint(jax.random.fold_in(_gk, 3), (200000,), 0, 12500, jnp.int32)
        _o = jnp.argsort(dst, stable=True)
        src = src[_o]
        dst = dst[_o]
        edge_attr_64 = -8.16379e-05 + 0.999858 * jax.random.normal(jax.random.fold_in(_gk, 12), (200000, 64), jnp.float32)
        edge_type_16 = jax.random.randint(jax.random.fold_in(_gk, 13), (200000,), 0, 16, jnp.int32)
        return (x, src, dst, edge_attr_64, edge_type_16)
    x, src, dst, edge_attr_64, edge_type_16 = _rec_inputs()

    def _L0_gnn_setup():
        import jax, jax.numpy as jnp
        import numpy as np
        N_NODES = 6250
        N_EDGES = 100000
        D_IN = 64
        D_OUT = 64
        NUM_RELS = 16
        key = jax.random.key(seed)
        k1, k2, k3, k4, k5 = jax.random.split(key, 5)
        feat = jax.random.normal(k1, (N_NODES, D_IN), dtype=jnp.float32)
        weight = jax.random.normal(k2, (NUM_RELS, D_IN, D_OUT), dtype=jnp.float32) * 0.05
        src = jax.random.randint(k3, (N_EDGES,), 0, N_NODES, dtype=jnp.int32)
        dst = jax.random.randint(k4, (N_EDGES,), 0, N_NODES, dtype=jnp.int32)
        etypes = jax.random.randint(k5, (N_EDGES,), 0, NUM_RELS, dtype=jnp.int32)
        return {'feat': feat, 'weight': weight, 'src': src, 'dst': dst, 'etypes': etypes}
    _L0_gnn_all = _L0_gnn_setup()
    _L0_gnn_in = {k: v for k, v in _L0_gnn_all.items() if k in ('weight',)}
    del _L0_gnn_all

    def _L1_gnn_setup():
        import jax, jax.numpy as jnp
        import numpy as np
        N_NODES = 12500
        N_EDGES = 200000
        D = 64

        def _segment_mean(data, segment_ids, num_segments):
            num = jax.ops.segment_sum(data, segment_ids, num_segments=num_segments)
            den = jax.ops.segment_sum(jnp.ones_like(data), segment_ids, num_segments=num_segments)
            return num / (1e-06 + den)
        key = jax.random.key(seed)
        ks = jax.random.split(key, 10)
        s = 1.0 / np.sqrt(D)
        return {'node_emb': jax.random.normal(ks[0], (N_NODES, D), jnp.float32), 'edge_emb': jax.random.normal(ks[1], (N_EDGES, D), jnp.float32), 'W1_msg': jax.random.normal(ks[2], (3 * D, D), jnp.float32) * s, 'b1_msg': jnp.zeros((D,), jnp.float32), 'W2_msg': jax.random.normal(ks[3], (D, D), jnp.float32) * s, 'b2_msg': jnp.zeros((D,), jnp.float32), 'W1_upd': jax.random.normal(ks[4], (2 * D, D), jnp.float32) * s, 'b1_upd': jnp.zeros((D,), jnp.float32), 'W2_upd': jax.random.normal(ks[5], (D, D), jnp.float32) * s, 'b2_upd': jnp.zeros((D,), jnp.float32), 'senders': jax.random.randint(ks[6], (N_EDGES,), 0, N_NODES), 'receivers': jax.random.randint(ks[7], (N_EDGES,), 0, N_NODES)}
    _L1_gnn_all = _L1_gnn_setup()
    _L1_gnn_in = {k: v for k, v in _L1_gnn_all.items() if k in ('W1_msg', 'b1_msg', 'W2_msg', 'b2_msg', 'W1_upd', 'b1_upd', 'W2_upd', 'b2_upd')}
    del _L1_gnn_all
    return {'x': x, 'src': src, 'dst': dst, 'edge_attr_64': edge_attr_64, 'edge_type_16': edge_type_16, 'L0_gnn_weight': _L0_gnn_in['weight'], 'L1_gnn_W1_msg': _L1_gnn_in['W1_msg'], 'L1_gnn_b1_msg': _L1_gnn_in['b1_msg'], 'L1_gnn_W2_msg': _L1_gnn_in['W2_msg'], 'L1_gnn_b2_msg': _L1_gnn_in['b2_msg'], 'L1_gnn_W1_upd': _L1_gnn_in['W1_upd'], 'L1_gnn_b1_upd': _L1_gnn_in['b1_upd'], 'L1_gnn_W2_upd': _L1_gnn_in['W2_upd'], 'L1_gnn_b2_upd': _L1_gnn_in['b2_upd']}

def reference(x, src, dst, edge_attr_64, edge_type_16, L0_gnn_weight, L1_gnn_W1_msg, L1_gnn_b1_msg, L1_gnn_W2_msg, L1_gnn_b2_msg, L1_gnn_W1_upd, L1_gnn_b1_upd, L1_gnn_W2_upd, L1_gnn_b2_upd):
    import jax
    import jax.numpy as jnp

    def _L0_gnn_ref(feat, weight, src, dst, etypes):
        import jax, jax.numpy as jnp
        import numpy as np
        N_NODES = 6250
        N_EDGES = 100000
        D_IN = 64
        D_OUT = 64
        NUM_RELS = 16
        num_rels = weight.shape[0]
        h_src = feat[src]
        msg = jnp.zeros((h_src.shape[0], weight.shape[2]), dtype=feat.dtype)
        for r in range(num_rels):
            mask = etypes == r
            msg = msg + h_src * mask[:, None].astype(feat.dtype) @ weight[r]
        out = jax.ops.segment_sum(msg, dst, num_segments=feat.shape[0])
        return out

    def _L1_gnn_ref(node_emb, edge_emb, W1_msg, b1_msg, W2_msg, b2_msg, W1_upd, b1_upd, W2_upd, b2_upd, senders, receivers):
        import jax, jax.numpy as jnp
        import numpy as np
        N_NODES = 12500
        N_EDGES = 200000
        D = 64

        def _segment_mean(data, segment_ids, num_segments):
            num = jax.ops.segment_sum(data, segment_ids, num_segments=num_segments)
            den = jax.ops.segment_sum(jnp.ones_like(data), segment_ids, num_segments=num_segments)
            return num / (1e-06 + den)
        sender_emb = node_emb[senders]
        receiver_emb = node_emb[receivers]
        msg_in = jnp.concatenate([edge_emb, sender_emb, receiver_emb], axis=-1)
        h = jax.nn.silu(msg_in @ W1_msg + b1_msg)
        edge_messages = h @ W2_msg + b2_msg
        node_messages = _segment_mean(edge_messages, receivers, node_emb.shape[0])
        upd_in = jnp.concatenate([node_emb, node_messages], axis=-1)
        hu = jax.nn.silu(upd_in @ W1_upd + b1_upd)
        new_node_emb = hu @ W2_upd + b2_upd
        return new_node_emb
    x = _layernorm(x + _L0_gnn_ref(x, L0_gnn_weight, src, dst, edge_type_16), axis=-1)
    x = _layernorm(x + _L1_gnn_ref(x, edge_attr_64, L1_gnn_W1_msg, L1_gnn_b1_msg, L1_gnn_W2_msg, L1_gnn_b2_msg, L1_gnn_W1_upd, L1_gnn_b1_upd, L1_gnn_W2_upd, L1_gnn_b2_upd, src, dst), axis=-1)
    return x

_drawn_inputs = setup_inputs


def setup_inputs(seed=0):
    import zlib

    import numpy as np

    out = dict(_drawn_inputs(seed))
    spreads = {'L1_gnn_b1_msg': (0.0, 0.29),
     'L1_gnn_b2_msg': (0.0, 0.1),
     'L1_gnn_b1_upd': (0.0, 0.1),
     'L1_gnn_b2_upd': (0.0, 0.1)}
    factors = {}
    for name, (base, spread) in spreads.items():
        noise = np.random.default_rng([zlib.crc32(name.encode()), seed]).standard_normal(out[name].shape)
        drawn = base * np.exp(spread * noise) if base else spread * noise
        out[name] = jnp.asarray(drawn.astype(out[name].dtype))
    for name, factor in factors.items():
        out[name] = (out[name] * factor).astype(out[name].dtype)
    return out
```

```python
from collections import namedtuple
from contextlib import ExitStack

import concourse.bass as bass
from concourse import mybir

F32 = mybir.dt.float32
BF16 = mybir.dt.bfloat16
I32 = mybir.dt.int32
ALU = mybir.AluOpType
ACT = mybir.ActivationFunctionType
AX_X = mybir.AxisListType.X

P = 128
T = 8
GE = P * T
W = 128
U = 4
EPS = 1e-5
EPS_MEAN = 1e-6

Turn = namedtuple("Turn", "n round slot")


def pipeline(eng, total, depth, step, unroll=U):
    def at_constant(i):
        def at(lag):
            n = i - lag
            return Turn(n, n // unroll, n % unroll) if 0 <= n < total else None
        return at

    def at_register(k, u):
        def at(lag):
            q, slot = divmod(u - lag, unroll)
            return Turn((k + q) * unroll + slot, k + q, slot)
        return at

    assert depth <= unroll
    rounds = total // unroll
    peeled = 4 // unroll
    for i in range(peeled * unroll):
        step(at_constant(i))
    with eng.Fori(peeled, rounds) as k:
        for u in range(unroll):
            step(at_register(k, u))
    for i in range(rounds * unroll, total + depth):
        step(at_constant(i))


def wait_from(eng, sem, turn, behind, unit=1):
    if isinstance(turn.n, int) and turn.n - behind + 1 <= 0:
        return
    eng.wait_ge(sem, (turn.n + (1 - behind)) * unit)


def gnn_kernel(nc, x_t, src_tab, dst_tab, type_tab, edge_t, w_rel, w_msg1, b_msg1, w_msg2_t,
               b_msg2, w_upd1, b_upd1, w_upd2, b_upd2, out):
    D, N = x_t.shape
    R = w_rel.shape[0]
    NG = src_tab.shape[1] // T
    E = edge_t.shape[1]
    assert E == NG * GE
    E_REAL = gnn_kernel.edges
    LAST = (E_REAL - (NG - 1) * GE) // T
    assert E_REAL % T == 0 and NG % U == 0
    NB = -(-N // (2 * P)) * 2
    NP = NB * P
    NC = NB // 2
    D1 = D + 1
    RD = R * D
    HALF = RD // 2

    y_tab = nc.dram_tensor("y_tab", (NP * R, D), F32).ap()
    p_tab = nc.dram_tensor("p_tab", (NP, D), F32).ap()
    q_tab = nc.dram_tensor("q_tab", (NP, D), F32).ap()

    with ExitStack() as ctx:
        def sb(name, shape, dt=F32):
            return ctx.enter_context(nc.sbuf_tensor(name, shape, dt))

        def sem(name):
            return ctx.enter_context(nc.semaphore(name))

        def sems(name, n):
            return [sem(f"{name}{i}") for i in range(n)]

        acc = sb("acc", [P, NP])
        x1u = sb("x1u", [P, NB, 2 * D])
        src_i = sb("src_i", [P, (NG + U) * T], I32)
        rel_i = sb("rel_i", [P, (NG + U) * T], I32)
        dst_i = sb("dst_i", [P, NG * T], I32)
        dloc = sb("dloc", [P, NG * T])
        spans = sb("spans", [P, 2 * NG])
        span_max = sb("span_max", [P, 2 * NG])
        base_f = sb("base_f", [P, NG])
        base_i = sb("base_i", [P, NG], I32)
        fits_f = sb("fits_f", [P, 1])
        fits_i = sb("fits_i", [P, 1], I32)
        past_end = sb("past_end", [P, T])
        idx = sb("idx", [P, U, T], I32)
        gat = sb("gat", [P, U, T, D1])
        onehot = sb("onehot", [P, U, GE])
        oh_bf = sb("oh_bf", [P, 2, GE], BF16)
        oh_t = sb("oh_t", [P, 2, GE])
        ea = sb("ea", [D1, U, GE])
        qwin = sb("qwin", [P, U, D])
        pre_s = sb("pre_s", [P, 2, T, D])
        h = sb("h", [P, 2, T, D1])
        xs = sb("xs", [D1, 2, 2 * P])
        pq = sb("pq", [P, 2, 2, 2 * D])
        sq = sb("sq", [P, D])
        ss = sb("ss", [P, 2, 2])
        var = sb("var", [P, 2, 2])
        rstd = sb("rstd", [P, 2, 2])
        mhalf = sb("mhalf", [P, 2])
        deg = sb("deg", [P, 2, 2])
        rinv = sb("rinv", [P, 2, 2])
        hu = sb("hu", [P, 2, 2, P])
        hu_t = sb("hu_t", [D1, 2, 2 * P])
        fin = sb("fin", [P, 2, 2, D])
        ident = sb("ident", [P, P])
        ident_bf = sb("ident_bf", [P, P], BF16)
        iota_s = sb("iota_s", [P, W])
        center = sb("center", [D, D])
        w_y = sb("w_y", [D, RD])
        w_ea = sb("w_ea", [D1, D])
        w_raw = sb("w_raw", [D, 4 * D])
        w_mid = sb("w_mid", [D1, 4 * D])
        w_m2t = sb("w_m2t", [D, D1])
        w_u1b = sb("w_u1b", [D, D])
        w_fin = sb("w_fin", [D1, D1])
        w_u2 = sb("w_u2", [D1, D])
        w_u2c = sb("w_u2c", [D1, D])
        mean_u2 = sb("mean_u2", [D1, 1])
        bias_u = sb("bias_u", [P, D])
        y_stage = onehot

        bank = [ctx.enter_context(nc.psum_tensor(f"bank{i}", [P, 512], F32)) for i in range(6)]
        bank_t = [ctx.enter_context(nc.psum_tensor(f"bank_t{i}", [P, GE], BF16)) for i in range(2)]
        seg = [bank[0], bank[1]]
        pre = [bank[2], bank[3]]

        s_const = sem("s_const")
        s_zero = sem("s_zero")
        s_x = sem("s_x")
        s_w = sem("s_w")
        s_tabs = sem("s_tabs")
        s_eye = sem("s_eye")
        s_iota = sem("s_iota")
        s_wps = sem("s_wps")
        s_wmid = sem("s_wmid")
        s_wfin = sem("s_wfin")
        s_prep = sem("s_prep")
        s_spans = sem("s_spans")
        s_allmax = sem("s_allmax")
        s_base = sem("s_base")
        y_x = sem("y_x")
        y_mm = sem("y_mm")
        y_ev0 = sem("y_ev0")
        y_ev1 = sem("y_ev1")
        y_out = sems("y_out", U)
        pool_turns = sem("pool_turns")
        r_idx = sem("r_idx")
        r_gat = sems("r_gat", U)
        r_hot = sem("r_hot")
        r_seg = sem("r_seg")
        r_acc = sem("r_acc")
        m_x = sem("m_x")
        m_mm = sem("m_mm")
        m_ss = sem("m_ss")
        m_var = sem("m_var")
        m_rstd = sem("m_rstd")
        m_pq = sem("m_pq")
        m_xu = sem("m_xu")
        m_u = sem("m_u")
        m_out = sems("m_out", 2)
        m_clear = sem("m_clear")
        e_idx = sem("e_idx")
        e_gat = sems("e_gat", U)
        e_ea = sems("e_ea", U)
        e_q = sems("e_q", U)
        e_hot = sem("e_hot")
        e_tr = sem("e_tr")
        e_oht = sem("e_oht")
        e_pre = sem("e_pre")
        e_sum = sem("e_sum")
        e_h = sem("e_h")
        e_seg = sem("e_seg")
        e_acc = sem("e_acc")
        g_idx = sem("g_idx")
        g_gat = sem("g_gat")
        g_cur = sem("g_cur")
        g_hot = sem("g_hot")
        g_seg = sem("g_seg")
        g_acc = sem("g_acc")
        g_ea = sem("g_ea")
        g_pre = sem("g_pre")
        g_sum = sem("g_sum")
        g_h = sem("g_h")
        f_x = sem("f_x")
        f_mm = sem("f_mm")
        f_deg = sem("f_deg")
        f_rinv = sem("f_rinv")
        f_t = sem("f_t")
        f_hu = sem("f_hu")
        f_tr = sem("f_tr")
        f_hut = sem("f_hut")
        f_z = sem("f_z")
        f_ss = sem("f_ss")
        f_var = sem("f_var")
        f_rstd = sem("f_rstd")
        f_fin = sem("f_fin")
        f_out = sems("f_out", 2)

        N_W = 11
        block = ctx.enter_context(nc.Block())

        def dloc_of(n):
            return dloc[:, bass.ds(n * T, T)]

        def window_onehot(eng, out_ap, d_ap):
            return eng.tensor_tensor(
                out_ap.rearrange("p (t w) -> p t w", t=T),
                bank[5][:, 0:W].rearrange("p (a w) -> p a w", a=1).to_broadcast([P, T, W]),
                d_ap.rearrange("p (t a) -> p t a", a=1).to_broadcast([P, T, W]), ALU.is_equal)

        def out_rows(c):
            return out[bass.ds(c * 2 * P, 2 * P), :].rearrange("(b p) f -> p b f", p=P)

        @block.sync
        def _(sp):
            sp.dma_start(acc[0:D, 0:N], x_t).then_inc(s_x, 16)
            sp.dma_start(w_y[:, :].rearrange("d (r f) -> d r f", r=R),
                         w_rel.rearrange("r d f -> d r f")).then_inc(s_x, 16)
            for tab, given in ((dst_i[:, :], dst_tab), (src_i[:, 0:NG * T], src_tab),
                               (rel_i[:, 0:NG * T], type_tab)):
                sp.dma_start(tab, given).then_inc(s_tabs, 16)
            sp.wait_ge(s_zero, 1)
            for to, of in ((w_ea[0:D, :], w_msg1[0:D, :]), (w_ea[D:D1, :], b_msg1),
                           (w_raw[:, 0:D], w_msg1[D:2 * D, :]), (w_raw[:, D:2 * D], w_msg1[2 * D:, :]),
                           (w_raw[:, 3 * D:4 * D], w_upd1[0:D, :]), (w_u1b[:, :], w_upd1[D:, :]),
                           (w_m2t[:, 0:D], w_msg2_t), (w_m2t[:, D:D1], b_msg2),
                           (w_u2[0:D, :], w_upd2), (w_u2[D:D1, :], b_upd2),
                           (bias_u[:, :], b_upd1.to_broadcast([P, D]))):
                sp.dma_start(to, of).then_inc(s_w, 16)

            def y_store(at):
                if t := at(0):
                    sp.wait_ge(y_ev0, t.n + 1)
                    sp.wait_ge(y_ev1, t.n + 1)
                    rows = y_tab[bass.ds(t.n * (P * R), P * R), :]
                    sp.dma_start(rows.rearrange("(p r) f -> p (r f)", p=P),
                                 y_stage[:, t.slot, :]).then_inc(y_out[t.slot], 16)
            pipeline(sp, NB, 0, y_store)

            def pq_store(at):
                if t := at(0):
                    sp.wait_ge(m_pq, t.n + 1)
                    for half, tab in enumerate((p_tab, q_tab)):
                        sp.dma_start(
                            tab[bass.ds(t.n * 2 * P, 2 * P), :].rearrange("(b p) f -> p b f", p=P),
                            pq[:, t.slot, :, half * D:(half + 1) * D]).then_inc(m_out[t.slot], 16)
            pipeline(sp, NC, 0, pq_store, 2)
            for s in range(2):
                sp.wait_ge(m_out[s], 32 * len(range(s, NC, 2)))
            sp.wait_ge(s_base, 1)

            def load_edges(sp_sem, slot, n):
                sp.dma_start(ea[0:D, slot, :], edge_t[:, bass.ds(n * GE, GE)]).then_inc(sp_sem, 16)

            fits = sp.value_load(fits_i[0:1, 0:1], min_val=0, max_val=1)
            with sp.If(fits > 0):
                def load(at):
                    if t := at(0):
                        wait_from(sp, e_pre, t, U)
                        load_edges(e_ea[t.slot], t.slot, t.n)
                        base = sp.value_load(base_i[0:1, bass.ds(t.n, 1)], min_val=0, max_val=NP - W)
                        sp.dma_start(qwin[:, t.slot, :], q_tab[bass.ds(base, W), :])\
                            .then_inc(e_q[t.slot], 16)
                pipeline(sp, NG, 0, load)
            with sp.Else():
                with sp.Fori(0, NG) as g:
                    sp.wait_ge(g_pre, g + 1)
                    load_edges(g_ea, 0, g)

            def store(at):
                if t := at(0):
                    sp.wait_ge(f_fin, t.n + 1)
                    if isinstance(t.n, int) and t.n == NC - 1:
                        for b in range(2):
                            first = (2 * t.n + b) * P
                            rows = max(0, min(P, N - first))
                            if rows:
                                sp.dma_start(out[first:first + rows, :], fin[0:rows, t.slot, b, :])\
                                    .then_inc(f_out[t.slot], 16)
                    else:
                        sp.dma_start(out_rows(t.n), fin[:, t.slot, :, :]).then_inc(f_out[t.slot], 16)
            pipeline(sp, NC, 0, store, 2)
            tail = (NC - 1) % 2
            parts = -(-(N - (NC - 1) * 2 * P) // P)
            for s in range(2):
                count = len(range(s, NC, 2)) + (parts - 1 if s == tail else 0)
                sp.wait_ge(f_out[s], 16 * count)

        @block.gpsimd
        def _(pool):
            pool.memset(ident[:, :], 0.0).then_inc(s_const, 1)
            pool.memset(center[:, :], -1.0 / D).then_inc(s_const, 1)
            pool.memset(mhalf[:, :], -0.5).then_inc(s_const, 1)
            pool.memset(past_end[:, :], 1e6).then_inc(s_const, 1)
            pool.iota(iota_s[:, :], [[1, W]], 0, 0, allow_small_or_imprecise_dtypes=True).then_inc(s_iota, 1)
            pool.wait_ge(s_const, 4)
            pool.affine_select(out=ident[:, :], in_=ident[:, :], compare_op=ALU.not_equal, fill=1.0,
                               base=0, pattern=[[-1, P]], channel_multiplier=1).then_inc(s_eye, 1)
            pool.affine_select(out=center[:, :], in_=center[:, :], compare_op=ALU.not_equal,
                               fill=1.0 - 1.0 / D, base=0, pattern=[[-1, D]],
                               channel_multiplier=1).then_inc(s_eye, 1)
            pool.affine_select(out=past_end[:, :], in_=past_end[:, :], compare_op=ALU.is_ge, fill=0.0,
                               base=-LAST, pattern=[[0, T]], channel_multiplier=1).then_inc(s_eye, 1)
            pool.wait_ge(s_eye, 3)
            pool.tensor_copy(ident_bf[:, :], ident[:, :]).then_inc(s_eye, 1)
            pool.wait_ge(s_spans, 2)
            pool.partition_all_reduce(span_max[:, :], spans[:, :], P, bass.bass_isa.ReduceOp.max)\
                .then_inc(s_allmax, 1)
            pool.wait_ge(s_base, 1)
            for s in range(U):
                pool.wait_ge(y_out[s], 16 * len(range(s, NB, U)))

            def gather(idx_sem, gat_sems, table):
                def step(at):
                    if t := at(0):
                        pool.wait_ge(idx_sem, t.n + 1)
                        pool.sem_inc(pool_turns, 1)
                        for j in range(T):
                            pool.indirect_dma_start(
                                gat[:, t.slot, j, 0:D], None, table,
                                bass.IndirectOffsetOnAxis(ap=idx[:, t.slot, j:j + 1], axis=0)
                            ).then_inc(gat_sems[t.slot], 16)
                return step

            def gather_whole(g, slot, table):
                for j in range(T):
                    pool.indirect_dma_start(
                        gat[:, slot, j, 0:D], None, table,
                        bass.IndirectOffsetOnAxis(ap=idx[:, slot, j:j + 1], axis=0)).then_inc(g_gat, 16)

            fits = pool.value_load(fits_i[0:1, 0:1], min_val=0, max_val=1)
            with pool.If(fits > 0):
                pipeline(pool, NG, 0, gather(r_idx, r_gat, y_tab))
            with pool.Else():
                with pool.Fori(0, NG) as g:
                    pool.wait_ge(g_idx, g + 1)
                    pool.sem_inc(pool_turns, 1)
                    gather_whole(g, 0, y_tab)

            def norm(t, ss_sem, var_sem, rstd_sem, used_sem):
                pool.wait_ge(ss_sem, 2 * (t.n + 1))
                wait_from(pool, used_sem, t, 2)
                pool.sem_inc(pool_turns, 1)
                pool.tensor_scalar(var[:, t.slot, :], ss[:, t.slot, :], 1.0 / D, EPS,
                                   ALU.mult, ALU.add).then_inc(var_sem, 1)
                pool.wait_ge(var_sem, t.n + 1)
                pool.tensor_tensor(rstd[:, t.slot, :], var[:, t.slot, :], mhalf[:, :], ALU.pow)\
                    .then_inc(rstd_sem, 1)

            def middle(at):
                if t := at(0):
                    norm(t, m_ss, m_var, m_rstd, m_xu)
                if t := at(1):
                    pool.wait_ge(m_xu, t.n + 1)
                    u = x1u[:, bass.ds(t.n * 2, 2), D:2 * D]
                    pool.tensor_tensor(u, u, bias_u[:, :].rearrange("p (a f) -> p a f", a=1)
                                       .to_broadcast([P, 2, D]), ALU.add).then_inc(m_u, 1)
            pipeline(pool, NC, 1, middle, 2)
            for s in range(2):
                pool.wait_ge(m_out[s], 32 * len(range(s, NC, 2)))
            with pool.If(fits > 0):
                pipeline(pool, NG, 0, gather(e_idx, e_gat, p_tab))
            with pool.Else():
                with pool.Fori(0, NG) as g:
                    pool.wait_ge(g_idx, NG + g + 1)
                    pool.sem_inc(pool_turns, 1)
                    gather_whole(g, 0, p_tab)
                    gather_whole(g, 1, q_tab)

            def end(at):
                if t := at(0):
                    norm(t, f_ss, f_var, f_rstd, f_fin)
            pipeline(pool, NC, 0, end, 2)

        @block.scalar
        def _(act):
            act.wait_ge(s_iota, 1)
            act.activation(bank[5][:, 0:W], iota_s[:, :], ACT.Copy).then_inc(s_iota, 1)
            act.wait_ge(s_x, 32)
            act.wait_ge(s_zero, 1)

            def stage_x(t, sem_, used, rows, cols):
                wait_from(act, used, t, 2)
                act.activation(xs[0:rows, t.slot % 2, 0:cols], acc[0:rows, bass.ds(t.n * cols, cols)],
                               ACT.Copy).then_inc(sem_, 1)

            def y_step(at):
                if t := at(0):
                    stage_x(t, y_x, y_mm, D, P)
                if t := at(1):
                    act.wait_ge(y_mm, t.n + 1)
                    if not (isinstance(t.n, int) and t.n < U):
                        act.wait_ge(y_out[t.slot], t.round * 16)
                    act.activation(y_stage[:, t.slot, 0:HALF], bank[2 * (t.slot % 2)][:, 0:HALF],
                                   ACT.Copy).then_inc(y_ev0, 1)
            pipeline(act, NB, 1, y_step)

            def squares(t, ps, cols, ready, ss_sem, used):
                act.wait_ge(ready, t.n + 1)
                wait_from(act, used, t, 2)
                for b in range(2):
                    if b or not isinstance(t.n, int) or t.n:
                        act.wait_ge(ss_sem, t.n * 2 + b)
                    act.activation(sq[:, :], ps[:, b * cols[2] + cols[0]:b * cols[2] + cols[1]],
                                   ACT.Square, accum_out=ss[:, t.slot, b:b + 1]).then_inc(ss_sem, 1)

            act.wait_ge(s_base, 1)
            fits = act.value_load(fits_i[0:1, 0:1], min_val=0, max_val=1)
            with act.If(fits > 0):
                act.wait_ge(r_acc, NG)
            with act.Else():
                act.wait_ge(g_acc, 1 + NG * NB)

            def middle(at):
                if t := at(0):
                    stage_x(t, m_x, m_mm, D1, 2 * P)
                if t := at(1):
                    squares(t, bank[2 + t.slot], (2 * D, 3 * D, 4 * D), m_mm, m_ss, m_var)
            pipeline(act, NC, 1, middle, 2)

            with act.If(fits > 0):
                def edge_step(at):
                    if t := at(0):
                        act.wait_ge(e_tr, t.n + 1)
                        wait_from(act, e_pre, t, 2)
                        act.activation(oh_t[:, t.slot % 2, :], bank_t[t.slot % 2][:, :], ACT.Copy)\
                            .then_inc(e_oht, 1)
                    if t := at(1):
                        act.wait_ge(e_sum, t.n + 1)
                        wait_from(act, e_seg, t, 2)
                        act.activation(h[:, t.slot % 2, :, 0:D], pre_s[:, t.slot % 2, :, :], ACT.Silu)\
                            .then_inc(e_h, 1)
                pipeline(act, NG, 1, edge_step)
                act.wait_ge(e_acc, NG)
            with act.Else():
                with act.Fori(0, NG) as g:
                    act.wait_ge(g_sum, g * 2 + 3)
                    act.wait_ge(g_acc, (g + NG) * NB + 1)
                    act.activation(h[:, 0, :, 0:D], pre_s[:, 0, :, :], ACT.Silu).then_inc(g_h, 1)
                act.wait_ge(g_acc, 1 + 2 * NG * NB)

            def end(at):
                if t := at(0):
                    stage_x(t, f_x, f_mm, D1, 2 * P)
                if t := at(1):
                    act.wait_ge(f_t, 2 * (t.n + 1))
                    wait_from(act, f_tr, t, 2)
                    act.activation(hu[:, t.slot, :, 0:D], pre_s[:, t.slot, 0:2, :], ACT.Silu)\
                        .then_inc(f_hu, 1)
                    act.wait_ge(f_tr, t.n + 1)
                    wait_from(act, f_z, t, 2)
                    act.activation(hu_t[:, t.slot, :], bank[2][0:D1, bass.ds(t.slot * 2 * P, 2 * P)],
                                   ACT.Copy).then_inc(f_hut, 1)
                if t := at(2):
                    squares(t, bank[3 + t.slot], (0, D, D), f_z, f_ss, f_var)
            pipeline(act, NC, 2, end, 2)

        @block.vector
        def _(dve):
            for tile in (acc[D:D1, :], src_i[:, NG * T:], rel_i[:, NG * T:],
                         w_mid[D:D1, :], w_fin[:, D:D1], hu[:, :, :, :]):
                dve.memset(tile, 0)
            dve.memset(acc[0:D, N:NP], 0)
            dve.memset(gat[:, :, :, D:D1], 1.0)
            dve.memset(h[:, :, :, D:D1], 1.0)
            dve.memset(ea[D:D1, :, :], 1.0).then_inc(s_prep, 1)
            dve.wait_ge(s_prep, 1)
            dve.memset(w_fin[D:D1, D:D1], 1.0)
            dve.memset(hu[:, :, :, D:D1], 1.0).then_inc(s_zero, 1)

            def y_step(at):
                if t := at(0):
                    dve.wait_ge(y_mm, t.n + 1)
                    if not (isinstance(t.n, int) and t.n < U):
                        dve.wait_ge(y_out[t.slot], t.round * 16)
                    dve.tensor_copy(y_stage[:, t.slot, HALF:RD], bank[2 * (t.slot % 2) + 1][:, 0:HALF])\
                        .then_inc(y_ev1, 1)

            d3 = dloc[:, :].rearrange("p (g t) -> p g t", t=T)
            dve.wait_ge(s_tabs, 48)
            dve.tensor_copy(dloc[:, :], dst_i[:, :]).then_inc(s_prep, 1)
            dve.scalar_tensor_tensor(rel_i[:, 0:NG * T], src_i[:, 0:NG * T], float(R),
                                     rel_i[:, 0:NG * T], ALU.mult, ALU.add)
            dve.wait_ge(s_prep, 2)
            dve.tensor_reduce(spans[:, 0:NG], d3, AX_X, ALU.min, negate=True).then_inc(s_spans, 1)
            dve.tensor_reduce(spans[:, NG:], d3, AX_X, ALU.max).then_inc(s_spans, 1)
            dve.wait_ge(s_w, 16 * N_W)
            dve.tensor_reduce(mean_u2[:, :], w_u2[:, :], AX_X, ALU.add).then_inc(s_prep, 1)
            dve.wait_ge(s_eye, 2)
            dve.tensor_copy(w_raw[:, 2 * D:3 * D], ident[0:D, 0:D]).then_inc(s_wmid, 1)
            dve.wait_ge(s_prep, 3)
            dve.tensor_scalar(mean_u2[:, :], mean_u2[:, :], -1.0 / D, None, ALU.mult).then_inc(s_prep, 1)
            dve.wait_ge(s_prep, 4)
            dve.tensor_scalar(w_u2c[:, :], w_u2[:, :], mean_u2[:, 0:1], None, ALU.add).then_inc(s_wfin, 1)
            dve.wait_ge(s_wps, 2)
            dve.tensor_copy(w_mid[0:D, :], bank[4][0:D, 0:4 * D]).then_inc(s_wmid, 1)
            dve.tensor_copy(w_fin[:, 0:D], bank[4][0:D1, 4 * D:5 * D]).then_inc(s_wfin, 1)
            pipeline(dve, NB, 0, y_step)

            dve.wait_ge(s_allmax, 1)
            dve.tensor_scalar(base_f[:, :], span_max[:, 0:NG], -1.0, float(NP - W), ALU.mult, ALU.min)\
                .then_inc(s_prep, 1)
            dve.wait_ge(s_prep, 5)
            dve.tensor_copy(base_i[:, :], base_f[:, :])
            dve.tensor_tensor(spans[:, 0:NG], span_max[:, NG:], base_f[:, :], ALU.subtract)\
                .then_inc(s_prep, 1)
            dve.tensor_tensor(d3, d3, base_f[:, :].rearrange("p (g a) -> p g a", a=1)
                              .to_broadcast([P, NG, T]), ALU.subtract).then_inc(s_prep, 1)
            dve.wait_ge(s_prep, 7)
            dve.tensor_reduce(fits_f[:, :], spans[:, 0:NG], AX_X, ALU.max).then_inc(s_prep, 1)
            last = dloc[:, (NG - 1) * T:]
            dve.wait_ge(s_eye, 3)
            dve.tensor_tensor(last, last, past_end[:, :], ALU.add).then_inc(s_prep, 1)
            dve.wait_ge(s_prep, 9)
            dve.tensor_scalar(fits_i[:, :], fits_f[:, :], float(W), None, ALU.is_lt).then_inc(s_base, 1)
            dve.wait_ge(s_base, 1)
            dve.wait_ge(s_iota, 2)
            dve.wait_ge(y_out[0], 16 * len(range(0, NB, U)))
            for s in range(1, U):
                dve.wait_ge(y_out[s], 16 * len(range(s, NB, U)))

            fits = dve.value_load(fits_i[0:1, 0:1], min_val=0, max_val=1)

            def put_idx(n, slot, table, sem_):
                dve.tensor_copy(idx[:, slot, :], table[:, bass.ds(n * T, T)]).then_inc(sem_, 1)

            def add_window(t, ps, rows, sem_):
                base = dve.value_load(base_i[0:1, bass.ds(t.n, 1)], min_val=0, max_val=NP - W)
                wait_from(dve, sem_, t, 1)
                win = acc[0:rows, bass.ds(base, W)]
                dve.tensor_tensor(win, ps[0:rows, 0:W], win, ALU.add).then_inc(sem_, 1)

            def windows(g, rows, first):
                cur = pre_s[:, 1, 0, 0:T]
                dve.tensor_scalar(cur, dloc_of(g), base_f[:, bass.ds(g, 1)], None, ALU.add)\
                    .then_inc(g_cur, 1)
                with dve.Fori(0, NB) as w:
                    done = (g + first) * NB + w
                    dve.wait_ge(g_cur, done + (g + first) + 1)
                    window_onehot(dve, onehot[:, 0, :], cur).then_inc(g_hot, 1)
                    dve.wait_ge(g_hot, done + 1)
                    dve.tensor_scalar(cur, cur, -float(W), None, ALU.add).then_inc(g_cur, 1)
                    dve.wait_ge(g_seg, done + 1)
                    win = acc[0:rows, bass.ds(w * W, W)]
                    dve.tensor_tensor(win, seg[0][0:rows, 0:W], win, ALU.add).then_inc(g_acc, 1)
                    dve.wait_ge(g_acc, done + 2)

            with dve.If(fits > 0):
                for s in range(U):
                    put_idx(s, s, rel_i, r_idx)

                def rel_step(at):
                    if t := at(0):
                        wait_from(dve, r_seg, t, U)
                        window_onehot(dve, onehot[:, t.slot, :], dloc_of(t.n)).then_inc(r_hot, 1)
                    if t := at(1):
                        dve.wait_ge(r_seg, t.n + 1)
                        put_idx(t.n + U, t.slot, rel_i, r_idx)
                        add_window(t, seg[t.slot % 2], D1, r_acc)
                pipeline(dve, NG, 1, rel_step)
            with dve.Else():
                dve.sem_inc(g_acc, 1)
                dve.sem_inc(g_sum, 1)
                with dve.Fori(0, NG) as g:
                    put_idx(g, 0, rel_i, g_idx)
                    windows(g, D1, 0)

            def middle(at):
                if t := at(0):
                    dve.wait_ge(m_rstd, t.n + 1)
                    if not (isinstance(t.n, int) and t.n < 2):
                        dve.wait_ge(m_out[t.slot], t.round * 32)
                    ps = bank[2 + t.slot][:, :].rearrange("p (b f) -> p b f", b=2)
                    r = rstd[:, t.slot, :].rearrange("p (b a) -> p b a", a=1).to_broadcast([P, 2, 2 * D])
                    dve.tensor_tensor(pq[:, t.slot, :, :], ps[:, :, 0:2 * D], r, ALU.mult)\
                        .then_inc(m_pq, 1)
                    dve.tensor_tensor(x1u[:, bass.ds(t.n * 2, 2), :], ps[:, :, 2 * D:], r, ALU.mult)\
                        .then_inc(m_xu, 1)
            pipeline(dve, NC, 0, middle, 2)
            dve.wait_ge(m_x, NC)
            dve.memset(acc[0:D, :], 0).then_inc(m_clear, 1)
            dve.wait_ge(m_clear, 1)

            with dve.If(fits > 0):
                for s in range(U):
                    put_idx(s, s, src_i, e_idx)

                def edge_step(at):
                    if t := at(0):
                        wait_from(dve, e_seg, t, U)
                        wait_from(dve, e_tr, t, 2)
                        window_onehot(dve, onehot[:, t.slot, :], dloc_of(t.n))
                        window_onehot(dve, oh_bf[:, t.slot % 2, :], dloc_of(t.n)).then_inc(e_hot, 1)
                    if t := at(1):
                        dve.wait_ge(e_pre, t.n + 1)
                        dve.wait_ge(e_gat[t.slot], (t.round + 1) * 16 * T)
                        wait_from(dve, e_h, t, 2)
                        dve.tensor_tensor(pre_s[:, t.slot % 2, :, :],
                                          pre[t.slot % 2][:, :].rearrange("p (t f) -> p t f", t=T),
                                          gat[:, t.slot, :, 0:D], ALU.add).then_inc(e_sum, 1)
                        dve.wait_ge(e_sum, t.n + 1)
                        put_idx(t.n + U, t.slot, src_i, e_idx)
                    if t := at(3):
                        dve.wait_ge(e_seg, t.n + 1)
                        add_window(t, seg[t.slot % 2], D, e_acc)
                pipeline(dve, NG, 3, edge_step)
            with dve.Else():
                with dve.Fori(0, NG) as g:
                    dve.tensor_copy(idx[:, 1, :], dst_i[:, bass.ds(g * T, T)])
                    put_idx(g, 0, src_i, g_idx)
                    dve.wait_ge(g_pre, g + 2)
                    dve.wait_ge(g_gat, g * (32 * T) + (NG * 16 * T + 32 * T))
                    dve.tensor_tensor(pre_s[:, 0, :, :],
                                      pre[0][:, :].rearrange("p (t f) -> p t f", t=T),
                                      gat[:, 0, :, 0:D], ALU.add).then_inc(g_sum, 1)
                    dve.wait_ge(g_sum, g * 2 + 2)
                    dve.tensor_tensor(pre_s[:, 0, :, :], pre_s[:, 0, :, :], gat[:, 1, :, 0:D],
                                      ALU.add).then_inc(g_sum, 1)
                    windows(g, D, NG)

            def end(at):
                if t := at(0):
                    dve.wait_ge(f_mm, t.n + 1)
                    wait_from(dve, f_hu, t, 2)
                    ps = bank[t.slot][:, 0:2 * D1].rearrange("p (b f) -> p b f", b=2)
                    dve.tensor_scalar(deg[:, t.slot, :], ps[:, :, D], EPS_MEAN, None, ALU.add)\
                        .then_inc(f_deg, 1)
                    dve.wait_ge(f_deg, t.n + 1)
                    dve.reciprocal(rinv[:, t.slot, :], deg[:, t.slot, :]).then_inc(f_rinv, 1)
                    dve.wait_ge(f_rinv, t.n + 1)
                    for b in range(2):
                        u = x1u[:, bass.ds(t.n * 2 + b, 1), D:2 * D].rearrange("p a f -> p (a f)")
                        dve.scalar_tensor_tensor(pre_s[:, t.slot, b, :], ps[:, b, 0:D],
                                                 rinv[:, t.slot, b:b + 1], u, ALU.mult, ALU.add)\
                            .then_inc(f_t, 1)
                if t := at(2):
                    dve.wait_ge(f_rstd, t.n + 1)
                    if not (isinstance(t.n, int) and t.n < 2):
                        dve.wait_ge(f_out[t.slot], t.round * 16)
                    ps = bank[3 + t.slot][:, 0:2 * D].rearrange("p (b f) -> p b f", b=2)
                    r = rstd[:, t.slot, :].rearrange("p (b a) -> p b a", a=1).to_broadcast([P, 2, D])
                    dve.tensor_tensor(fin[:, t.slot, :, :], ps, r, ALU.mult).then_inc(f_fin, 1)
            dve.wait_ge(m_u, NC)
            pipeline(dve, NC, 2, end, 2)

        @block.tensor
        def _(pe):
            pe.wait_ge(s_w, 16 * N_W)
            pe.wait_ge(s_eye, 3)
            pe.wait_ge(s_wmid, 1)
            pe.matmul(bank[4][0:D, 0:4 * D], center[:, :], w_raw[:, :], start=True, stop=True)\
                .then_inc(s_wps, 1)
            pe.matmul(bank[4][0:D1, 4 * D:5 * D], w_m2t[:, :], w_u1b[:, :], start=True, stop=True)\
                .then_inc(s_wps, 1)
            pe.wait_ge(s_x, 32)

            def y_step(at):
                if t := at(0):
                    pe.wait_ge(y_x, t.n + 1)
                    wait_from(pe, y_ev0, t, 2)
                    wait_from(pe, y_ev1, t, 2)
                    s = t.slot % 2
                    for half in range(2):
                        mm = pe.matmul(bank[2 * s + half][:, 0:HALF], xs[0:D, s, 0:P],
                                       w_y[:, half * HALF:(half + 1) * HALF], start=True, stop=True)
                    mm.then_inc(y_mm, 1)
            pipeline(pe, NB, 0, y_step)

            def segment_sums(ps, rows, hot):
                for j in range(T):
                    mm = pe.matmul(ps[0:D1, 0:W], rows[:, j, :], hot[:, j * W:(j + 1) * W],
                                   start=(j == 0), stop=(j == T - 1))
                return mm

            def windows(g, rows, first, rows_sem, rows_there):
                with pe.Fori(0, NB) as w:
                    done = (g + first) * NB + w
                    pe.wait_ge(rows_sem, rows_there)
                    pe.wait_ge(g_hot, done + 1)
                    pe.wait_ge(g_acc, done + 1)
                    segment_sums(seg[0], rows, onehot[:, 0, :]).then_inc(g_seg, 1)

            pe.wait_ge(s_base, 1)
            fits = pe.value_load(fits_i[0:1, 0:1], min_val=0, max_val=1)
            with pe.If(fits > 0):
                def rel_step(at):
                    if t := at(0):
                        pe.wait_ge(r_hot, t.n + 1)
                        pe.wait_ge(r_gat[t.slot], (t.round + 1) * 16 * T)
                        wait_from(pe, r_acc, t, 2)
                        segment_sums(seg[t.slot % 2], gat[:, t.slot, :, :], onehot[:, t.slot, :])\
                            .then_inc(r_seg, 1)
                pipeline(pe, NG, 0, rel_step)
            with pe.Else():
                pe.sem_inc(g_pre, 1)
                with pe.Fori(0, NG) as g:
                    windows(g, gat[:, 0, :, :], 0, g_gat, (g + 1) * (16 * T))

            pe.wait_ge(s_wmid, 2)

            def middle(at):
                if t := at(0):
                    pe.wait_ge(m_x, t.n + 1)
                    wait_from(pe, m_xu, t, 2)
                    for b in range(2):
                        mm = pe.matmul(bank[2 + t.slot][:, b * 4 * D:(b + 1) * 4 * D],
                                       xs[:, t.slot, b * P:(b + 1) * P], w_mid[:, :],
                                       start=True, stop=True)
                    mm.then_inc(m_mm, 1)
            pipeline(pe, NC, 0, middle, 2)
            pe.wait_ge(m_xu, NC)

            with pe.If(fits > 0):
                def edge_step(at):
                    if t := at(0):
                        pe.wait_ge(e_hot, t.n + 1)
                        wait_from(pe, e_oht, t, 2)
                        for j in range(T):
                            mm = pe.transpose(bank_t[t.slot % 2][:, j * P:(j + 1) * P],
                                              oh_bf[:, t.slot % 2, j * W:(j + 1) * W], ident_bf[:, :])
                        mm.then_inc(e_tr, 1)
                    if t := at(1):
                        pe.wait_ge(e_oht, t.n + 1)
                        pe.wait_ge(e_ea[t.slot], (t.round + 1) * 16)
                        pe.wait_ge(e_q[t.slot], (t.round + 1) * 16)
                        wait_from(pe, e_sum, t, 2)
                        for j in range(T):
                            o = pre[t.slot % 2][:, j * D:(j + 1) * D]
                            pe.matmul(o, ea[:, t.slot, j * P:(j + 1) * P], w_ea[:, :],
                                      start=True, stop=False)
                            mm = pe.matmul(o, oh_t[:, t.slot % 2, j * P:(j + 1) * P],
                                           qwin[:, t.slot, :], start=False, stop=True)
                        mm.then_inc(e_pre, 1)
                    if t := at(2):
                        pe.wait_ge(e_h, t.n + 1)
                        wait_from(pe, e_acc, t, 2)
                        segment_sums(seg[t.slot % 2], h[:, t.slot % 2, :, :], onehot[:, t.slot, :])\
                            .then_inc(e_seg, 1)
                pipeline(pe, NG, 2, edge_step)
            with pe.Else():
                with pe.Fori(0, NG) as g:
                    pe.wait_ge(g_ea, (g + 1) * 16)
                    pe.wait_ge(g_sum, g * 2 + 1)
                    for j in range(T):
                        mm = pe.matmul(pre[0][:, j * D:(j + 1) * D], ea[:, 0, j * P:(j + 1) * P],
                                       w_ea[:, :], start=True, stop=True)
                    mm.then_inc(g_pre, 1)
                    windows(g, h[:, 0, :, :], NG, g_h, g + 1)

            pe.wait_ge(s_wfin, 2)

            def end(at):
                if t := at(0):
                    pe.wait_ge(f_x, t.n + 1)
                    wait_from(pe, f_t, t, 2, 2)
                    for b in range(2):
                        mm = pe.matmul(bank[t.slot][:, b * D1:(b + 1) * D1],
                                       xs[:, t.slot, b * P:(b + 1) * P], w_fin[:, :],
                                       start=True, stop=True)
                    mm.then_inc(f_mm, 1)
                if t := at(1):
                    pe.wait_ge(f_hu, t.n + 1)
                    wait_from(pe, f_hut, t, 2)
                    for b in range(2):
                        mm = pe.transpose(bank[2][:, t.slot * 2 * P + b * P:t.slot * 2 * P + (b + 1) * P],
                                          hu[:, t.slot, b, :], ident[:, :])
                    mm.then_inc(f_tr, 1)
                    pe.wait_ge(f_hut, t.n + 1)
                    wait_from(pe, f_fin, t, 2)
                    for b in range(2):
                        o = bank[3 + t.slot][:, b * D:(b + 1) * D]
                        pe.matmul(o, hu_t[:, t.slot, b * P:(b + 1) * P], w_u2c[:, :],
                                  start=True, stop=False)
                        x1 = x1u[:, bass.ds(t.n * 2 + b, 1), 0:D].rearrange("p a f -> p (a f)")
                        mm = pe.matmul(o, ident[:, :], x1, start=False, stop=True)
                    mm.then_inc(f_z, 1)
            pipeline(pe, NC, 1, end, 2)


def kernel(x, src, dst, edge_attr_64, edge_type_16, L0_gnn_weight, L1_gnn_W1_msg, L1_gnn_b1_msg,
           L1_gnn_W2_msg, L1_gnn_b2_msg, L1_gnn_W1_upd, L1_gnn_b1_upd, L1_gnn_W2_upd, L1_gnn_b2_upd):
    import numpy as np
    import concourse.bacc as bacc
    from concourse.bass_utils import run_bass_kernel_spmd

    edges, nodes, d = src.shape[0], x.shape[0], x.shape[1]
    groups = -(-edges // GE)
    fill = groups * GE - edges

    def by_partition(a):
        a = np.asarray(a)
        a = np.concatenate([a, np.repeat(a[-1:], fill)])
        return np.ascontiguousarray(a.reshape(groups, P, T).transpose(1, 0, 2)).reshape(P, groups * T)

    def rows(a):
        return np.ascontiguousarray(a).reshape(1, -1)

    e = np.asarray(edge_attr_64)
    e = np.concatenate([e, np.repeat(e[-1:], fill, axis=0)])
    e = np.ascontiguousarray(e.reshape(groups, P, T, d).transpose(3, 0, 2, 1)).reshape(d, groups * GE)
    given = [
        ("x_t", np.ascontiguousarray(np.asarray(x).T)), ("src_tab", by_partition(src)),
        ("dst_tab", by_partition(dst)), ("type_tab", by_partition(edge_type_16)), ("edge_t", e),
        ("w_rel", np.ascontiguousarray(L0_gnn_weight)), ("w_msg1", np.ascontiguousarray(L1_gnn_W1_msg)),
        ("b_msg1", rows(L1_gnn_b1_msg)), ("w_msg2_t", np.ascontiguousarray(np.asarray(L1_gnn_W2_msg).T)),
        ("b_msg2", np.ascontiguousarray(L1_gnn_b2_msg).reshape(-1, 1)),
        ("w_upd1", np.ascontiguousarray(L1_gnn_W1_upd)), ("b_upd1", rows(L1_gnn_b1_upd)),
        ("w_upd2", np.ascontiguousarray(L1_gnn_W2_upd)), ("b_upd2", rows(L1_gnn_b2_upd)),
    ]
    nc = bacc.Bacc("TRN2", target_bir_lowering=False, num_devices=1)
    args = [nc.dram_tensor(name, a.shape, mybir.dt.from_np(a.dtype), kind="ExternalInput").ap()
            for name, a in given]
    out = nc.dram_tensor("new_x", (nodes, d), F32, kind="ExternalOutput").ap()
    gnn_kernel.edges = edges
    gnn_kernel(nc, *args, out)
    r = run_bass_kernel_spmd(nc, [dict(given)], core_ids=[0])
    return r.results[0]["new_x"]
```

```python
from collections import namedtuple
from contextlib import ExitStack

import concourse.bass as bass
from concourse import mybir

F32 = mybir.dt.float32
BF16 = mybir.dt.bfloat16
I32 = mybir.dt.int32
ALU = mybir.AluOpType
ACT = mybir.ActivationFunctionType
AX_X = mybir.AxisListType.X

P = 128
T = 8
GE = P * T
W = 128
U = 4
EPS = 1e-5
EPS_MEAN = 1e-6

Turn = namedtuple("Turn", "n round slot")


def pipeline(eng, total, depth, step, unroll=U, peeled=1):
    def at_constant(i):
        def at(lag):
            n = i - lag
            return Turn(n, n // unroll, n % unroll) if 0 <= n < total else None
        return at

    def at_register(k, u):
        def at(lag):
            q, slot = divmod(u - lag, unroll)
            return Turn((k + q) * unroll + slot, k + q, slot)
        return at

    assert depth <= unroll * peeled and peeled < total // unroll
    rounds = total // unroll
    for i in range(peeled * unroll):
        step(at_constant(i))
    with eng.Fori(peeled, rounds) as k:
        for u in range(unroll):
            step(at_register(k, u))
    for i in range(rounds * unroll, total + depth):
        step(at_constant(i))


def chunk_of(turn):
    return Turn(turn.round, turn.round, 0) if turn and turn.slot == 0 else None


def wait_from(eng, sem, turn, behind, unit=1):
    if isinstance(turn.n, int) and turn.n - behind + 1 <= 0:
        return
    eng.wait_ge(sem, (turn.n + (1 - behind)) * unit)


def gnn_kernel(nc, x_t, src_tab, dst_tab, type_tab, edge_t, w_rel, w_msg1, b_msg1, w_msg2_t,
               b_msg2, w_upd1, b_upd1, w_upd2, b_upd2, out):
    D, N = x_t.shape
    R = w_rel.shape[0]
    NG = src_tab.shape[1] // T
    E = edge_t.shape[1]
    assert E == NG * GE
    E_REAL = gnn_kernel.edges
    LAST = (E_REAL - (NG - 1) * GE) // T
    assert E_REAL % T == 0 and NG % U == 0
    NB = -(-N // (2 * P)) * 2
    NP = NB * P
    NC = NB // 2
    assert NC == NG // U
    D1 = D + 1
    RD = R * D
    HALF = RD // 2

    y_tab = nc.dram_tensor("y_tab", (NP * R, D), F32).ap()
    p_tab = nc.dram_tensor("p_tab", (NP, D), F32).ap()
    q_tab = nc.dram_tensor("q_tab", (NP, 3 * D), BF16).ap()

    with ExitStack() as ctx:
        def sb(name, shape, dt=F32):
            return ctx.enter_context(nc.sbuf_tensor(name, shape, dt))

        def sem(name):
            return ctx.enter_context(nc.semaphore(name))

        def sems(name, n):
            return [sem(f"{name}{i}") for i in range(n)]

        acc = sb("acc", [P, NP])
        x1u = sb("x1u", [P, NB, 2 * D])
        src_i = sb("src_i", [P, (NG + U) * T], I32)
        rel_i = sb("rel_i", [P, (NG + U) * T], I32)
        dst_i = sb("dst_i", [P, NG * T], I32)
        dloc = sb("dloc", [P, NG * T])
        spans = sb("spans", [P, 2 * NG])
        span_max = sb("span_max", [P, 2 * NG])
        done_to = sb("done_to", [P, NG])
        base_f = sb("base_f", [P, NG])
        base_i = sb("base_i", [P, NG], I32)
        fits_f = sb("fits_f", [P, 1])
        fits_i = sb("fits_i", [P, 1], I32)
        past_end = sb("past_end", [P, T])
        cur = sb("cur", [P, T])
        idx = sb("idx", [P, U, T], I32)
        gat = sb("gat", [P, U, T, D1])
        onehot = sb("onehot", [P, U, GE])
        oh_t = sb("oh_t", [P, 2, GE], BF16)
        ea = sb("ea", [P, U, GE])
        qwin = sb("qwin", [P, U, 3 * D], BF16)
        r = sb("r", [P, U, T * D])
        h3 = sb("h3", [P, U, 3, T * D], BF16)
        seg_s = sb("seg_s", [P, P])
        xs = sb("xs", [D1, 2 * P])
        p_st = sb("p_st", [P, 2, D])
        q_f = sb("q_f", [P, 2, D])
        q_st = sb("q_st", [P, 2, 3, D], BF16)
        sq = sb("sq", [P, D])
        ss = sb("ss", [P, 2])
        std = sb("std", [P, 2])
        rstd = sb("rstd", [P, 2])
        eps = sb("eps", [P, 1])
        zero = sb("zero", [D, 1])
        deg = sb("deg", [P, 2])
        rinv = sb("rinv", [P, 2])
        pre_u = sb("pre_u", [P, 2, D])
        hu = sb("hu", [P, 2, P])
        hu_t = sb("hu_t", [D1, 2 * P])
        fin = sb("fin", [P, 2, D])
        ident = sb("ident", [P, P])
        ident_bf = sb("ident_bf", [P, P], BF16)
        iota_s = sb("iota_s", [P, W])
        center = sb("center", [D, D])
        w_ea = sb("w_ea", [D1, D])
        w_raw = sb("w_raw", [D, 4 * D])
        w_mid = sb("w_mid", [D1, 4 * D])
        w_m2t = sb("w_m2t", [D, D1])
        w_u1b = sb("w_u1b", [D, D])
        w_fin = sb("w_fin", [D1, D1])
        w_u2 = sb("w_u2", [D1, D])
        w_u2c = sb("w_u2c", [D1, D])
        mean_u2 = sb("mean_u2", [D1, 1])
        bias_u = sb("bias_u", [P, D])

        y_stage = onehot
        x_in, x_rest = r[:, :, 0:P], r[:, :, P:2 * P]
        x_h = h3[:, :, 0, 0:P]
        x_m = h3[:, :, 0, P:2 * P]
        x_lh = h3[:, :, 0, 2 * P:3 * P]
        w_y, w_rest = ea[:, 0, :], ea[:, 1, :]
        w_high = ea[:, 2, :].bitcast(BF16)[:, 0:RD]
        w_hm = ea[:, 2, :].bitcast(BF16)[:, RD:2 * RD]
        w_hl = ea[:, 3, :].bitcast(BF16)[:, 0:RD]
        hot_bf = onehot[:, :, :].rearrange("p u w -> p (u w)").bitcast(BF16)

        bank = [ctx.enter_context(nc.psum_tensor(f"bank{i}", [P, 512], F32)) for i in range(6)]
        bank_t = [ctx.enter_context(nc.psum_tensor(f"bank_t{i}", [P, GE], BF16)) for i in range(2)]
        seg = [bank[0], bank[1]]
        seg_n, seg_f = bank[0], bank[1]
        pre = [bank[2], bank[3]]
        nodes = bank[4]
        iota = bank[5]

        s_const = sem("s_const")
        s_zero = sem("s_zero")
        s_ones = sem("s_ones")
        s_x = sem("s_x")
        s_wy = sem("s_wy")
        s_w = sem("s_w")
        s_tabs = sem("s_tabs")
        s_eye = sem("s_eye")
        s_iota = sem("s_iota")
        s_wps = sem("s_wps")
        s_wmid = sem("s_wmid")
        s_wfin = sem("s_wfin")
        s_whigh = sem("s_whigh")
        s_wrest = sem("s_wrest")
        s_wmiddle = sem("s_wmiddle")
        s_wlow = sem("s_wlow")
        s_prep = sem("s_prep")
        s_spans = sem("s_spans")
        s_allmax = sem("s_allmax")
        s_base = sem("s_base")
        y_in = sems("y_in", U)
        y_hi = sem("y_hi")
        y_rest = sem("y_rest")
        y_md = sem("y_md")
        y_lo = sem("y_lo")
        y_mm = sem("y_mm")
        y_ev0 = sem("y_ev0")
        y_ev1 = sem("y_ev1")
        y_out = sems("y_out", U)
        pool_turns = sem("pool_turns")
        r_idx = sem("r_idx")
        r_gat = sems("r_gat", U)
        r_hot = sem("r_hot")
        r_seg = sem("r_seg")
        r_acc = sem("r_acc")
        m_x = sem("m_x")
        m_mm = sem("m_mm")
        m_ss = sem("m_ss")
        m_std = sem("m_std")
        m_rstd = sem("m_rstd")
        m_read = sem("m_read")
        m_split = sem("m_split")
        m_out = sem("m_out")
        m_clear = sem("m_clear")
        e_idx = sem("e_idx")
        e_gat = sems("e_gat", U)
        e_ea = sems("e_ea", U)
        e_q = sems("e_q", U)
        e_hot = sem("e_hot")
        e_tr = sem("e_tr")
        e_oht = sem("e_oht")
        e_pre = sem("e_pre")
        e_sum = sem("e_sum")
        e_hi = sem("e_hi")
        e_h = sem("e_h")
        e_rest = sem("e_rest")
        e_md = sem("e_md")
        e_lo = sem("e_lo")
        e_seg = sem("e_seg")
        e_segs = sem("e_segs")
        e_segt = sem("e_segt")
        e_acc = sem("e_acc")
        g_idx = sem("g_idx")
        g_gat = sem("g_gat")
        g_cur = sem("g_cur")
        g_hot = sem("g_hot")
        g_seg = sem("g_seg")
        g_acc = sem("g_acc")
        g_ea = sem("g_ea")
        g_pre = sem("g_pre")
        g_sum = sem("g_sum")
        g_h = sem("g_h")
        f_x = sem("f_x")
        f_mm = sem("f_mm")
        f_deg = sem("f_deg")
        f_rinv = sem("f_rinv")
        f_pre = sem("f_pre")
        f_hu = sem("f_hu")
        f_tr = sem("f_tr")
        f_hut = sem("f_hut")
        f_z = sem("f_z")
        f_ss = sem("f_ss")
        f_std = sem("f_std")
        f_rstd = sem("f_rstd")
        f_fin = sem("f_fin")
        f_out = sem("f_out")

        N_W = 11
        N_SUM = 4
        TR, PRE, REST, SEG, ADD, NODE = 1, 2, 3, 4, 5, 11
        STORE = 16
        block = ctx.enter_context(nc.Block())

        def dloc_of(n):
            return dloc[:, bass.ds(n * T, T)]

        def window_onehot(eng, out_ap, d_ap):
            return eng.tensor_tensor(
                out_ap.rearrange("p (t w) -> p t w", t=T),
                iota[:, 0:W].rearrange("p (a w) -> p a w", a=1).to_broadcast([P, T, W]),
                d_ap.rearrange("p (t a) -> p t a", a=1).to_broadcast([P, T, W]), ALU.is_equal)

        last_chunk = Turn(NC - 1, NC - 1, 0)

        def hot_slot(t):
            return hot_bf[:, t.slot * GE:(t.slot + 1) * GE]

        def gathered_q(j):
            return h3[:, 1, :, :].rearrange("p k f -> p (k f)")[:, j * 3 * D:(j + 1) * 3 * D]

        def by_block(ap):
            return ap.rearrange("p (b f) -> p b f", b=2)

        @block.sync
        def _(sp):
            for half in range(2):
                sp.dma_start(w_y[half * D:(half + 1) * D, :].rearrange("d (r f) -> d r f", r=R),
                             w_rel.rearrange("r d f -> d r f")).then_inc(s_wy, 16)

            def y_step(at):
                if t := at(0):
                    cols = min(P, N - t.n * P) if isinstance(t.n, int) else P
                    wait_from(sp, y_rest, t, U)
                    for half in range(2):
                        sp.dma_start(x_in[half * D:(half + 1) * D, t.slot, 0:cols],
                                     x_t[:, bass.ds(t.n * P, cols)]).then_inc(y_in[t.slot], 16)
                if t := at(4):
                    sp.wait_ge(y_ev0, t.n + 1)
                    sp.wait_ge(y_ev1, t.n + 1)
                    rows = y_tab[bass.ds(t.n * (P * R), P * R), :]
                    sp.dma_start(rows.rearrange("(p r) f -> p (r f)", p=P),
                                 y_stage[:, t.slot, :]).then_inc(y_out[t.slot], 16)
                    if isinstance(t.n, int) and t.n == 0:
                        rest_of_loads()

            def rest_of_loads():
                for tab, given in ((dst_i[:, :], dst_tab), (src_i[:, 0:NG * T], src_tab),
                                   (rel_i[:, 0:NG * T], type_tab)):
                    sp.dma_start(tab, given).then_inc(s_tabs, 16)
                for to, of in ((w_ea[0:D, :], w_msg1[0:D, :]), (w_ea[D:D1, :], b_msg1),
                               (w_raw[:, 0:D], w_msg1[D:2 * D, :]),
                               (w_raw[:, D:2 * D], w_msg1[2 * D:, :]),
                               (w_raw[:, 3 * D:4 * D], w_upd1[0:D, :]), (w_u1b[:, :], w_upd1[D:, :]),
                               (w_m2t[:, 0:D], w_msg2_t), (w_m2t[:, D:D1], b_msg2),
                               (w_u2[0:D, :], w_upd2), (w_u2[D:D1, :], b_upd2),
                               (bias_u[:, :], b_upd1.to_broadcast([P, D]))):
                    sp.dma_start(to, of).then_inc(s_w, 16)
                sp.dma_start(acc[0:D, 0:N], x_t).then_inc(s_x, 16)
            pipeline(sp, NB, 4, y_step, peeled=2)

            def pq_store(at):
                if t := at(0):
                    sp.wait_ge(m_split, 4 * (t.n + 1))
                    sp.dma_start(
                        p_tab[bass.ds(t.n * 2 * P, 2 * P), :].rearrange("(b p) f -> p b f", p=P),
                        p_st[:, :, :]).then_inc(m_out, 16)
                    sp.dma_start(
                        q_tab[bass.ds(t.n * 2 * P, 2 * P), :].rearrange("(b p) f -> p b f", p=P),
                        q_st[:, :, :, :].rearrange("p b k f -> p b (k f)")).then_inc(m_out, 16)
            pipeline(sp, NC, 0, pq_store, 1)
            sp.wait_ge(m_out, 32 * NC)
            sp.wait_ge(s_ones, 1)

            def load_edges(sem_, slot, n):
                sp.dma_start(ea[0:D, slot, :], edge_t[:, bass.ds(n * GE, GE)]).then_inc(sem_, 16)

            parts = -(-(N - (NC - 1) * 2 * P) // P)

            def store(t):
                sp.wait_ge(f_fin, t.n + 1)
                if isinstance(t.n, int) and t.n == NC - 1:
                    for b in range(parts):
                        first = (2 * t.n + b) * P
                        rows = min(P, N - first)
                        sp.dma_start(out[first:first + rows, :], fin[0:rows, b, :]).then_inc(f_out, 16)
                else:
                    sp.dma_start(out[bass.ds(t.n * 2 * P, 2 * P), :].rearrange("(b p) f -> p b f", p=P),
                                 fin[:, :, :]).then_inc(f_out, 16)

            fits = sp.value_load(fits_i[0:1, 0:1], min_val=0, max_val=1)
            with sp.If(fits > 0):
                def edge_step(at):
                    if t := at(0):
                        wait_from(sp, e_pre, t, U)
                        load_edges(e_ea[t.slot], t.slot, t.n)
                        base = sp.value_load(base_i[0:1, bass.ds(t.n, 1)], min_val=0, max_val=NP - W)
                        sp.dma_start(qwin[:, t.slot, :], q_tab[bass.ds(base, W), :])\
                            .then_inc(e_q[t.slot], 16)
                    if t := chunk_of(at(STORE)):
                        store(t)
                pipeline(sp, NG, STORE, edge_step, peeled=STORE // U)
            with sp.Else():
                with sp.Fori(0, NG) as g:
                    sp.wait_ge(g_pre, g + 1)
                    load_edges(g_ea, 0, g)
                pipeline(sp, NC - 1, 0, lambda at: store(at(0)), 1)
                store(last_chunk)
            sp.wait_ge(f_out, 16 * (NC - 1 + parts))

        @block.gpsimd
        def _(pool):
            pool.memset(ident[:, :], 0.0).then_inc(s_const, 1)
            pool.memset(center[:, :], -1.0 / D).then_inc(s_const, 1)
            pool.memset(past_end[:, :], 1e6).then_inc(s_const, 1)
            pool.memset(eps[:, :], EPS).then_inc(s_const, 1)
            pool.iota(iota_s[:, :], [[1, W]], 0, 0, allow_small_or_imprecise_dtypes=True).then_inc(s_iota, 1)
            lim = done_to[:, :].rearrange("p (k u) -> p k u", u=U)
            pool.iota(lim, [[2 * P, NG // U], [0, U]], -2 * P, 0,
                      allow_small_or_imprecise_dtypes=True).then_inc(s_const, 1)
            pool.wait_ge(s_const, 5)
            pool.iota(lim[:, :, U - 1:U], [[2 * P, NG // U], [0, 1]], 0, 0,
                      allow_small_or_imprecise_dtypes=True).then_inc(s_const, 1)
            pool.affine_select(out=ident[:, :], in_=ident[:, :], compare_op=ALU.not_equal, fill=1.0,
                               base=0, pattern=[[-1, P]], channel_multiplier=1).then_inc(s_eye, 1)
            pool.affine_select(out=center[:, :], in_=center[:, :], compare_op=ALU.not_equal,
                               fill=1.0 - 1.0 / D, base=0, pattern=[[-1, D]],
                               channel_multiplier=1).then_inc(s_eye, 1)
            pool.affine_select(out=past_end[:, :], in_=past_end[:, :], compare_op=ALU.is_ge, fill=0.0,
                               base=-LAST, pattern=[[0, T]], channel_multiplier=1).then_inc(s_eye, 1)
            pool.wait_ge(s_eye, 3)
            pool.tensor_copy(ident_bf[:, :], ident[:, :]).then_inc(s_eye, 1)
            pool.wait_ge(s_eye, 4)
            pool.wait_ge(s_const, 6)

            def y_step(at):
                if t := at(0):
                    pool.wait_ge(y_in[t.slot], (t.round + 1) * 32)
                    wait_from(pool, y_mm, t, U)
                    pool.sem_inc(pool_turns, 1)
                    pool.tensor_copy(x_h[:, t.slot, :], x_in[:, t.slot, :]).then_inc(y_hi, 1)
            pipeline(pool, NB, 0, y_step)
            pool.wait_ge(s_spans, 2)
            pool.partition_all_reduce(span_max[:, :], spans[:, :], P, bass.bass_isa.ReduceOp.max)\
                .then_inc(s_allmax, 1)
            pool.wait_ge(s_base, 1)
            for s in range(U):
                pool.wait_ge(y_out[s], 16 * len(range(s, NB, U)))

            def gather(idx_sem, gat_sems, table):
                def step(at):
                    if t := at(0):
                        pool.wait_ge(idx_sem, t.n + 1)
                        pool.sem_inc(pool_turns, 1)
                        for j in range(T):
                            pool.indirect_dma_start(
                                gat[:, t.slot, j, 0:D], None, table,
                                bass.IndirectOffsetOnAxis(ap=idx[:, t.slot, j:j + 1], axis=0)
                            ).then_inc(gat_sems[t.slot], 16)
                return step

            def gather_whole(slot, to, table):
                for j in range(T):
                    pool.indirect_dma_start(
                        to(j), None, table,
                        bass.IndirectOffsetOnAxis(ap=idx[:, slot, j:j + 1], axis=0)).then_inc(g_gat, 16)

            fits = pool.value_load(fits_i[0:1, 0:1], min_val=0, max_val=1)
            with pool.If(fits > 0):
                pipeline(pool, NG, 0, gather(r_idx, r_gat, y_tab))
            with pool.Else():
                with pool.Fori(0, NG) as g:
                    pool.wait_ge(g_idx, g + 1)
                    pool.sem_inc(pool_turns, 1)
                    gather_whole(0, lambda j: gat[:, 0, j, 0:D], y_tab)

            pool.wait_ge(m_out, 32 * NC)
            with pool.If(fits > 0):
                pipeline(pool, NG, 0, gather(e_idx, e_gat, p_tab))
            with pool.Else():
                with pool.Fori(0, NG) as g:
                    pool.wait_ge(g_idx, NG + g + 1)
                    pool.sem_inc(pool_turns, 1)
                    gather_whole(0, lambda j: gat[:, 0, j, 0:D], p_tab)
                    gather_whole(1, gathered_q, q_tab)

        @block.scalar
        def _(act):
            act.wait_ge(s_iota, 1)
            act.activation(iota[:, 0:W], iota_s[:, :], ACT.Copy).then_inc(s_iota, 1)
            act.wait_ge(s_wy, 32)
            act.activation(w_high[D:P, :], w_y[D:P, :], ACT.Copy).then_inc(s_whigh, 1)
            act.activation(w_hm[0:D, :], w_y[0:D, :], ACT.Copy)
            act.activation(w_hl[0:D, :], w_y[0:D, :], ACT.Copy)
            act.wait_ge(s_wrest, 1)
            act.activation(w_hm[D:P, :], w_rest[D:P, :], ACT.Copy).then_inc(s_wmiddle, 1)

            def y_step(at):
                if t := at(1):
                    act.wait_ge(y_rest, t.n + 1)
                    wait_from(act, y_mm, t, U)
                    act.activation(x_m[:, t.slot, :], x_rest[:, t.slot, :], ACT.Copy).then_inc(y_md, 1)
                    act.activation(x_lh[D:P, t.slot, :], x_h[D:P, t.slot, :], ACT.Copy)\
                        .then_inc(y_md, 1)
                if t := at(3):
                    act.wait_ge(y_mm, t.n + 1)
                    if not (isinstance(t.n, int) and t.n < U):
                        act.wait_ge(y_out[t.slot], t.round * 16)
                    act.activation(y_stage[:, t.slot, 0:HALF], bank[2 * (t.slot % 2)][:, 0:HALF],
                                   ACT.Copy).then_inc(y_ev0, 1)
            pipeline(act, NB, 3, y_step, peeled=2)

            def stage_x(t, sem_, used):
                wait_from(act, used, t, 1)
                act.activation(xs[:, :], acc[0:D1, bass.ds(t.n * 2 * P, 2 * P)], ACT.Copy)\
                    .then_inc(sem_, 1)

            def deviation(t, first, stride, ready, ss_sem, std_sem, used):
                act.wait_ge(ready, t.n + 1)
                for b in range(2):
                    if b or not isinstance(t.n, int) or t.n:
                        act.wait_ge(ss_sem, t.n * 2 + b)
                    act.activation(sq[:, :], nodes[:, first + b * stride:first + b * stride + D],
                                   ACT.Square, accum_out=ss[:, b:b + 1]).then_inc(ss_sem, 1)
                act.wait_ge(ss_sem, (t.n + 1) * 2)
                wait_from(act, used, t, 1)
                act.activation(std[:, :], ss[:, :], ACT.Sqrt, bias=eps[:, 0:1], scale=1.0 / D)\
                    .then_inc(std_sem, 1)

            act.wait_ge(s_base, 1)
            act.wait_ge(s_zero, 1)
            act.wait_ge(s_const, 6)

            def middle(at):
                if t := at(0):
                    act.wait_ge(r_acc, min(U * t.n + U + 3, NG) if isinstance(t.n, int)
                                else t.n * U + (U + 3))
                    stage_x(t, m_x, m_mm)
                    deviation(t, 2 * D, 4 * D, m_mm, m_ss, m_std, m_rstd)
            pipeline(act, NC - 1, 0, middle, 1, peeled=2)
            middle(lambda lag: last_chunk)

            def node_a(t):
                stage_x(t, f_x, f_mm)

            def node_b(t):
                act.wait_ge(f_pre, 2 * (t.n + 1))
                wait_from(act, f_tr, t, 1)
                act.activation(hu[:, :, 0:D], pre_u[:, :, :], ACT.Silu).then_inc(f_hu, 1)
                act.wait_ge(f_tr, t.n + 1)
                wait_from(act, f_z, t, 1)
                act.activation(hu_t[:, :], nodes[0:D1, 0:2 * P], ACT.Copy).then_inc(f_hut, 1)
                deviation(t, 2 * P, D, f_z, f_ss, f_std, f_rstd)

            fits = act.value_load(fits_i[0:1, 0:1], min_val=0, max_val=1)
            with act.If(fits > 0):
                def edge_step(at):
                    if t := at(TR):
                        act.wait_ge(e_tr, t.n + 1)
                        wait_from(act, e_pre, t, 2)
                        act.activation(oh_t[:, t.slot % 2, :], bank_t[t.slot % 2][:, :], ACT.Copy)\
                            .then_inc(e_oht, 1)
                    if t := at(REST):
                        act.wait_ge(e_rest, t.n + 1)
                        act.activation(h3[:, t.slot, 1, :], r[:, t.slot, :], ACT.Copy)\
                            .then_inc(e_md, 1)
                    if t := at(PRE):
                        act.wait_ge(e_sum, t.n + 1)
                        wait_from(act, e_seg, t, U)
                        act.activation(h3[:, t.slot, 0, :], r[:, t.slot, :], ACT.Silu)\
                            .then_inc(e_hi, 1)
                        act.activation(r[:, t.slot, :], r[:, t.slot, :], ACT.Silu).then_inc(e_h, 1)
                    if t := at(SEG):
                        act.wait_ge(e_seg, t.n + 1)
                        wait_from(act, e_segt, t, 1)
                        act.activation(seg_s[:, 0:D], seg_n[:, 0:D], ACT.Copy).then_inc(e_segs, 1)
                    if t := chunk_of(at(NODE)):
                        act.wait_ge(e_acc, min(U * t.n + U + 3, NG) if isinstance(t.n, int)
                                    else t.n * U + (U + 3))
                        node_a(t)
                    if t := chunk_of(at(NODE + 1)):
                        node_b(t)
                pipeline(act, NG, NODE + 1, edge_step, peeled=4)
            with act.Else():
                with act.Fori(0, NG) as g:
                    act.wait_ge(g_sum, g * N_SUM + N_SUM + 1)
                    act.wait_ge(g_acc, (g + NG) * NB + 1)
                    act.activation(r[:, 1, :], r[:, 0, :], ACT.Silu).then_inc(g_h, 1)
                act.wait_ge(g_acc, 1 + 2 * NG * NB)

                def end(at):
                    node_a(at(0))
                    node_b(at(0))
                pipeline(act, NC, 0, end, 1)

        @block.vector
        def _(dve):
            dve.wait_ge(s_whigh, 1)
            dve.tensor_tensor(w_rest[D:P, :], w_y[D:P, :], w_high[D:P, :], ALU.subtract)\
                .then_inc(s_wrest, 1)
            dve.memset(src_i[:, NG * T:], 0)
            dve.memset(rel_i[:, NG * T:], 0)
            dve.memset(w_mid[D:D1, :], 0)
            dve.memset(w_fin[:, D:D1], 0)
            dve.memset(hu[:, :, :], 0)
            dve.memset(seg_s[:, :], 0)
            dve.memset(zero[:, :], 0)
            dve.memset(acc[D:D1, :], 0)
            dve.memset(acc[0:D, N:NP], 0)
            dve.memset(gat[:, :, :, D:D1], 1.0).then_inc(s_prep, 1)
            dve.wait_ge(s_prep, 1)
            dve.memset(w_fin[D:D1, D:D1], 1.0)
            dve.memset(hu[:, :, D:D1], 1.0).then_inc(s_zero, 1)
            dve.wait_ge(s_wmiddle, 1)
            dve.tensor_tensor(w_hl[D:P, :], w_rest[D:P, :], w_hm[D:P, :], ALU.subtract)\
                .then_inc(s_wlow, 1)

            def y_step(at):
                if t := at(0):
                    dve.wait_ge(y_hi, t.n + 1)
                    wait_from(dve, y_lo, t, U)
                    dve.tensor_tensor(x_rest[:, t.slot, :], x_in[:, t.slot, :], x_h[:, t.slot, :],
                                      ALU.subtract).then_inc(y_rest, 1)
                if t := at(1):
                    dve.wait_ge(y_md, 2 * (t.n + 1))
                    dve.tensor_tensor(x_lh[0:D, t.slot, :], x_rest[0:D, t.slot, :],
                                      x_m[0:D, t.slot, :], ALU.subtract).then_inc(y_lo, 1)
                if t := at(3):
                    dve.wait_ge(y_mm, t.n + 1)
                    if not (isinstance(t.n, int) and t.n < U):
                        dve.wait_ge(y_out[t.slot], t.round * 16)
                    dve.tensor_copy(y_stage[:, t.slot, HALF:RD], bank[2 * (t.slot % 2) + 1][:, 0:HALF])\
                        .then_inc(y_ev1, 1)
                    if isinstance(t.n, int) and t.n == 4:
                        prepare()

            d3 = dloc[:, :].rearrange("p (g t) -> p g t", t=T)

            def prepare():
                dve.wait_ge(s_tabs, 48)
                dve.tensor_copy(dloc[:, :], dst_i[:, :]).then_inc(s_prep, 1)
                dve.scalar_tensor_tensor(rel_i[:, 0:NG * T], src_i[:, 0:NG * T], float(R),
                                         rel_i[:, 0:NG * T], ALU.mult, ALU.add)
                dve.wait_ge(s_prep, 2)
                dve.tensor_reduce(spans[:, 0:NG], d3, AX_X, ALU.min, negate=True).then_inc(s_spans, 1)
                dve.tensor_reduce(spans[:, NG:], d3, AX_X, ALU.max).then_inc(s_spans, 1)
                dve.wait_ge(s_w, 16 * N_W)
                dve.tensor_reduce(mean_u2[:, :], w_u2[:, :], AX_X, ALU.add).then_inc(s_prep, 1)
                dve.wait_ge(s_eye, 2)
                dve.tensor_copy(w_raw[:, 2 * D:3 * D], ident[0:D, 0:D]).then_inc(s_wmid, 1)
                dve.wait_ge(s_prep, 3)
                dve.tensor_scalar(mean_u2[:, :], mean_u2[:, :], -1.0 / D, None, ALU.mult).then_inc(s_prep, 1)
                dve.wait_ge(s_prep, 4)
                dve.tensor_scalar(w_u2c[:, :], w_u2[:, :], mean_u2[:, 0:1], None, ALU.add).then_inc(s_wfin, 1)
            pipeline(dve, NB, 3, y_step, peeled=2)

            dve.wait_ge(y_mm, NB)
            dve.memset(ea[D:D1, :, :], 1.0).then_inc(s_ones, 1)

            dve.wait_ge(s_allmax, 1)
            dve.tensor_scalar(base_f[:, :], span_max[:, 0:NG], -1.0, float(NP - W), ALU.mult, ALU.min)\
                .then_inc(s_prep, 1)
            dve.wait_ge(s_prep, 5)
            dve.tensor_copy(base_i[:, :], base_f[:, :])
            dve.wait_ge(s_const, 6)
            dve.scalar_tensor_tensor(spans[:, 0:NG], span_max[:, NG:], -float(W), base_f[:, :],
                                     ALU.add, ALU.subtract)
            dve.scalar_tensor_tensor(spans[:, NG:], done_to[:, :], -0.5, base_f[:, :],
                                     ALU.add, ALU.subtract).then_inc(s_prep, 1)
            dve.tensor_tensor(d3, d3, base_f[:, :].rearrange("p (g a) -> p g a", a=1)
                              .to_broadcast([P, NG, T]), ALU.subtract).then_inc(s_prep, 1)
            dve.wait_ge(s_prep, 7)
            dve.tensor_reduce(fits_f[:, :], spans[:, :], AX_X, ALU.max).then_inc(s_prep, 1)
            last = dloc[:, (NG - 1) * T:]
            dve.wait_ge(s_eye, 3)
            dve.tensor_tensor(last, last, past_end[:, :], ALU.add).then_inc(s_prep, 1)
            dve.wait_ge(s_prep, 9)
            dve.tensor_scalar(fits_i[:, :], fits_f[:, :], 0.0, None, ALU.is_lt).then_inc(s_base, 1)
            dve.wait_ge(s_wps, 2)
            dve.tensor_copy(w_mid[0:D, :], nodes[0:D, 0:4 * D]).then_inc(s_wmid, 1)
            dve.tensor_copy(w_fin[:, 0:D], nodes[0:D1, 4 * D:5 * D]).then_inc(s_wfin, 1)
            dve.wait_ge(s_base, 1)
            dve.wait_ge(s_iota, 2)
            dve.wait_ge(s_x, 16)
            for s in range(U):
                dve.wait_ge(y_out[s], 16 * len(range(s, NB, U)))

            fits = dve.value_load(fits_i[0:1, 0:1], min_val=0, max_val=1)

            def put_idx(n, slot, table, sem_):
                dve.tensor_copy(idx[:, slot, :], table[:, bass.ds(n * T, T)]).then_inc(sem_, 1)

            def add_window(t, ps, rows, sem_):
                base = dve.value_load(base_i[0:1, bass.ds(t.n, 1)], min_val=0, max_val=NP - W)
                wait_from(dve, sem_, t, 1)
                win = acc[0:rows, bass.ds(base, W)]
                dve.tensor_tensor(win, ps[0:rows, 0:W], win, ALU.add).then_inc(sem_, 1)

            def windows(g, rows, first):
                dve.tensor_scalar(cur[:, :], dloc_of(g), base_f[:, bass.ds(g, 1)], None, ALU.add)\
                    .then_inc(g_cur, 1)
                with dve.Fori(0, NB) as w:
                    done = (g + first) * NB + w
                    dve.wait_ge(g_cur, done + (g + first) + 1)
                    window_onehot(dve, onehot[:, 0, :], cur[:, :]).then_inc(g_hot, 1)
                    dve.wait_ge(g_hot, done + 1)
                    dve.tensor_scalar(cur[:, :], cur[:, :], -float(W), None, ALU.add)\
                        .then_inc(g_cur, 1)
                    dve.wait_ge(g_seg, done + 1)
                    win = acc[0:rows, bass.ds(w * W, W)]
                    dve.tensor_tensor(win, seg[0][0:rows, 0:W], win, ALU.add).then_inc(g_acc, 1)
                    dve.wait_ge(g_acc, done + 2)

            def over_features(ap):
                return ap.rearrange("p (b a) -> p b a", a=1).to_broadcast([P, 2, D])

            def middle(t):
                dve.wait_ge(m_std, t.n + 1)
                wait_from(dve, m_read, t, 1)
                dve.reciprocal(rstd[:, :], std[:, :]).then_inc(m_rstd, 1)
                dve.wait_ge(m_rstd, t.n + 1)
                if not (isinstance(t.n, int) and t.n == 0):
                    dve.wait_ge(m_out, t.n * 32)
                ps = by_block(nodes[:, :])
                scale = over_features(rstd[:, :])
                x1 = x1u[:, bass.ds(t.n * 2, 2), 0:D]
                dve.tensor_tensor(q_f[:, :, :], ps[:, :, D:2 * D], scale, ALU.mult).then_inc(m_split, 1)
                dve.tensor_tensor(p_st[:, :, :], ps[:, :, 0:D], scale, ALU.mult)
                dve.tensor_tensor(x1, ps[:, :, 2 * D:3 * D], scale, ALU.mult)
                for b in range(2):
                    u = x1u[:, bass.ds(t.n * 2 + b, 1), D:2 * D].rearrange("p a f -> p (a f)")
                    ins = dve.scalar_tensor_tensor(u, ps[:, b, 3 * D:4 * D], rstd[:, b:b + 1],
                                                   bias_u[:, :], ALU.mult, ALU.add)
                ins.then_inc(m_read, 1)
                dve.wait_ge(m_split, t.n * 4 + 1)
                dve.tensor_copy(q_st[:, :, 0, :], q_f[:, :, :]).then_inc(m_split, 1)
                dve.wait_ge(m_split, t.n * 4 + 2)
                dve.tensor_tensor(q_f[:, :, :], q_f[:, :, :], q_st[:, :, 0, :], ALU.subtract)\
                    .then_inc(m_clear, 1)
                dve.wait_ge(m_clear, t.n * 2 + 1)
                dve.tensor_copy(q_st[:, :, 1, :], q_f[:, :, :]).then_inc(m_split, 1)
                dve.tensor_copy(acc[0:D, bass.ds(t.n * 2 * P, 2 * P)],
                                zero[:, :].to_broadcast([D, 2 * P])).then_inc(m_clear, 1)
                dve.wait_ge(m_split, t.n * 4 + 3)
                dve.tensor_tensor(q_st[:, :, 2, :], q_f[:, :, :], q_st[:, :, 1, :], ALU.subtract)\
                    .then_inc(m_split, 1)

            with dve.If(fits > 0):
                for s in range(U):
                    put_idx(s, s, rel_i, r_idx)

                def rel_step(at):
                    if t := at(0):
                        wait_from(dve, r_seg, t, U)
                        window_onehot(dve, onehot[:, t.slot, :], dloc_of(t.n)).then_inc(r_hot, 1)
                    if t := at(1):
                        dve.wait_ge(r_seg, t.n + 1)
                        put_idx(t.n + U, t.slot, rel_i, r_idx)
                        add_window(t, seg[t.slot % 2], D1, r_acc)
                    if t := chunk_of(at(9)):
                        middle(t)
                pipeline(dve, NG, 9, rel_step, peeled=3)
            with dve.Else():
                dve.sem_inc(g_acc, 1)
                dve.sem_inc(g_sum, 1)
                with dve.Fori(0, NG) as g:
                    put_idx(g, 0, rel_i, g_idx)
                    windows(g, D1, 0)
                dve.sem_inc(r_acc, NG)
                pipeline(dve, NC, 0, lambda at: middle(at(0)), 1, peeled=2)
            dve.wait_ge(m_clear, 2 * NC)

            def node_a(t):
                dve.wait_ge(f_mm, t.n + 1)
                ps = by_block(nodes[:, 0:2 * D1])
                dve.tensor_scalar(deg[:, :], ps[:, :, D], EPS_MEAN, None, ALU.add).then_inc(f_deg, 1)
                dve.wait_ge(f_deg, t.n + 1)
                wait_from(dve, f_pre, t, 1, 2)
                dve.reciprocal(rinv[:, :], deg[:, :]).then_inc(f_rinv, 1)
                dve.wait_ge(f_rinv, t.n + 1)
                wait_from(dve, f_hu, t, 1)
                for b in range(2):
                    u = x1u[:, bass.ds(t.n * 2 + b, 1), D:2 * D].rearrange("p a f -> p (a f)")
                    dve.scalar_tensor_tensor(pre_u[:, b, :], ps[:, b, 0:D], rinv[:, b:b + 1], u,
                                             ALU.mult, ALU.add).then_inc(f_pre, 1)

            def node_c(t):
                dve.wait_ge(f_std, t.n + 1)
                wait_from(dve, f_fin, t, 1)
                dve.reciprocal(rstd[:, :], std[:, :]).then_inc(f_rstd, 1)
                dve.wait_ge(f_rstd, t.n + 1)
                if not (isinstance(t.n, int) and t.n == 0):
                    dve.wait_ge(f_out, t.n * 16)
                dve.tensor_tensor(fin[:, :, :], by_block(nodes[:, 2 * P:2 * P + 2 * D]),
                                  over_features(rstd[:, :]), ALU.mult).then_inc(f_fin, 1)

            with dve.If(fits > 0):
                for s in range(U):
                    put_idx(s, s, src_i, e_idx)

                def edge_step(at):
                    if t := at(SEG):
                        dve.wait_ge(e_md, t.n + 1)
                        dve.tensor_tensor(h3[:, t.slot, 2, :], r[:, t.slot, :], h3[:, t.slot, 1, :],
                                          ALU.subtract).then_inc(e_lo, 1)
                    if t := at(REST):
                        dve.wait_ge(e_h, t.n + 1)
                        dve.tensor_tensor(r[:, t.slot, :], r[:, t.slot, :], h3[:, t.slot, 0, :],
                                          ALU.subtract).then_inc(e_rest, 1)
                    if t := at(ADD):
                        dve.wait_ge(e_segt, t.n + 1)
                        add_window(t, seg_f, D, e_acc)
                    if t := at(PRE):
                        dve.wait_ge(e_pre, t.n + 1)
                        dve.wait_ge(e_gat[t.slot], (t.round + 1) * 16 * T)
                        wait_from(dve, e_lo, t, U)
                        dve.tensor_tensor(r[:, t.slot, :].rearrange("p (t f) -> p t f", t=T),
                                          pre[t.slot % 2][:, :].rearrange("p (t f) -> p t f", t=T),
                                          gat[:, t.slot, :, 0:D], ALU.add).then_inc(e_sum, 1)
                        dve.wait_ge(e_sum, t.n + 1)
                        put_idx(t.n + U, t.slot, src_i, e_idx)
                    if t := at(0):
                        wait_from(dve, e_seg, t, U)
                        window_onehot(dve, hot_slot(t), dloc_of(t.n)).then_inc(e_hot, 1)
                    if t := chunk_of(at(NODE)):
                        node_a(t)
                    if t := chunk_of(at(NODE + 2)):
                        node_c(t)
                pipeline(dve, NG, NODE + 2, edge_step, peeled=4)
            with dve.Else():
                with dve.Fori(0, NG) as g:
                    dve.tensor_copy(idx[:, 1, :], dst_i[:, bass.ds(g * T, T)])
                    put_idx(g, 0, src_i, g_idx)
                    dve.wait_ge(g_pre, g + 2)
                    dve.wait_ge(g_gat, g * (32 * T) + (NG * 16 * T + 32 * T))
                    to = r[:, 0, :].rearrange("p (t f) -> p t f", t=T)
                    q3 = h3[:, 1, :, :].rearrange("p k f -> p (k f)").rearrange(
                        "p (t k f) -> p t k f", t=T, k=3)
                    before = pre[0][:, :].rearrange("p (t f) -> p t f", t=T)
                    for k, more in enumerate((gat[:, 0, :, 0:D], q3[:, :, 0, :], q3[:, :, 1, :],
                                              q3[:, :, 2, :])):
                        if k:
                            dve.wait_ge(g_sum, g * N_SUM + (k + 1))
                        dve.tensor_tensor(to, before, more, ALU.add).then_inc(g_sum, 1)
                        before = to
                    windows(g, D, NG)

                def end(at):
                    node_a(at(0))
                    node_c(at(0))
                pipeline(dve, NC, 0, end, 1, peeled=2)

        @block.tensor
        def _(pe):
            pe.wait_ge(s_wlow, 1)

            def y_step(at):
                if t := at(2):
                    pe.wait_ge(y_lo, t.n + 1)
                    wait_from(pe, y_ev0, t, 2)
                    wait_from(pe, y_ev1, t, 2)
                    for half in range(2):
                        o = bank[2 * (t.slot % 2) + half][:, 0:HALF]
                        cols = slice(half * HALF, (half + 1) * HALF)
                        parts = ((x_h, w_hm), (x_m, w_hm), (x_lh, w_hl))
                        for k, (xp, wp) in enumerate(parts):
                            mm = pe.matmul(o, xp[:, t.slot, :], wp[:, cols], start=(k == 0),
                                           stop=(k == len(parts) - 1))
                    mm.then_inc(y_mm, 1)
            pipeline(pe, NB, 2, y_step)

            pe.wait_ge(s_w, 16 * N_W)
            pe.wait_ge(s_eye, 4)
            pe.wait_ge(s_wmid, 1)
            pe.wait_ge(s_zero, 1)
            pe.matmul(nodes[0:D, 0:4 * D], center[:, :], w_raw[:, :], start=True, stop=True)\
                .then_inc(s_wps, 1)
            pe.matmul(nodes[0:D1, 4 * D:5 * D], w_m2t[:, :], w_u1b[:, :], start=True, stop=True)\
                .then_inc(s_wps, 1)

            def segment_sums(ps, rows, width, hot):
                for j in range(T):
                    mm = pe.matmul(ps[0:width, 0:W], rows[:, j, :], hot[:, j * W:(j + 1) * W],
                                   start=(j == 0), stop=(j == T - 1))
                return mm

            def windows(g, rows, width, first, rows_sem, rows_there):
                with pe.Fori(0, NB) as w:
                    done = (g + first) * NB + w
                    pe.wait_ge(rows_sem, rows_there)
                    pe.wait_ge(g_hot, done + 1)
                    pe.wait_ge(g_acc, done + 1)
                    segment_sums(seg[0], rows, width, onehot[:, 0, :]).then_inc(g_seg, 1)

            def middle(t):
                pe.wait_ge(m_x, t.n + 1)
                wait_from(pe, m_read, t, 1)
                for b in range(2):
                    mm = pe.matmul(nodes[:, b * 4 * D:(b + 1) * 4 * D], xs[:, b * P:(b + 1) * P],
                                   w_mid[:, :], start=True, stop=True)
                mm.then_inc(m_mm, 1)

            pe.wait_ge(s_base, 1)
            pe.wait_ge(s_wmid, 2)
            pe.wait_ge(s_wfin, 2)
            fits = pe.value_load(fits_i[0:1, 0:1], min_val=0, max_val=1)
            with pe.If(fits > 0):
                def rel_step(at):
                    if t := at(0):
                        pe.wait_ge(r_hot, t.n + 1)
                        pe.wait_ge(r_gat[t.slot], (t.round + 1) * 16 * T)
                        wait_from(pe, r_acc, t, 2)
                        segment_sums(seg[t.slot % 2], gat[:, t.slot, :, :], D1, onehot[:, t.slot, :])\
                            .then_inc(r_seg, 1)
                    if t := chunk_of(at(8)):
                        middle(t)
                pipeline(pe, NG, 8, rel_step, peeled=3)
            with pe.Else():
                pe.sem_inc(g_pre, 1)
                with pe.Fori(0, NG) as g:
                    windows(g, gat[:, 0, :, :], D1, 0, g_gat, (g + 1) * (16 * T))
                pipeline(pe, NC, 0, lambda at: middle(at(0)), 1, peeled=2)
            pe.wait_ge(m_read, NC)

            def node_a(t):
                pe.wait_ge(f_x, t.n + 1)
                wait_from(pe, f_fin, t, 1)
                for b in range(2):
                    mm = pe.matmul(nodes[:, b * D1:(b + 1) * D1], xs[:, b * P:(b + 1) * P],
                                   w_fin[:, :], start=True, stop=True)
                mm.then_inc(f_mm, 1)

            def node_b(t):
                pe.wait_ge(f_hu, t.n + 1)
                for b in range(2):
                    mm = pe.transpose(nodes[:, b * P:(b + 1) * P], hu[:, b, :], ident[:, :])
                mm.then_inc(f_tr, 1)
                pe.wait_ge(f_hut, t.n + 1)
                for b in range(2):
                    o = nodes[:, 2 * P + b * D:2 * P + (b + 1) * D]
                    pe.matmul(o, hu_t[:, b * P:(b + 1) * P], w_u2c[:, :], start=True, stop=False)
                    x1 = x1u[:, bass.ds(t.n * 2 + b, 1), 0:D].rearrange("p a f -> p (a f)")
                    mm = pe.matmul(o, ident[:, :], x1, start=False, stop=True)
                mm.then_inc(f_z, 1)

            with pe.If(fits > 0):
                def edge_step(at):
                    if t := at(TR):
                        pe.wait_ge(e_hot, t.n + 1)
                        wait_from(pe, e_oht, t, 2)
                        hot = hot_slot(t)
                        for j in range(T):
                            mm = pe.transpose(bank_t[t.slot % 2][:, j * P:(j + 1) * P],
                                              hot[:, j * W:(j + 1) * W], ident_bf[:, :])
                        mm.then_inc(e_tr, 1)
                    if t := at(ADD):
                        pe.wait_ge(e_segs, t.n + 1)
                        wait_from(pe, e_acc, t, 1)
                        pe.transpose(seg_f[:, 0:P], seg_s[:, :], ident[:, :]).then_inc(e_segt, 1)
                    if t := at(PRE):
                        pe.wait_ge(e_oht, t.n + 1)
                        pe.wait_ge(e_ea[t.slot], (t.round + 1) * 16)
                        pe.wait_ge(e_q[t.slot], (t.round + 1) * 16)
                        wait_from(pe, e_sum, t, 2)
                        for j in range(T):
                            o = pre[t.slot % 2][:, j * D:(j + 1) * D]
                            pe.matmul(o, ea[0:D1, t.slot, j * P:(j + 1) * P], w_ea[:, :],
                                      start=True, stop=False)
                            for k in range(3):
                                mm = pe.matmul(o, oh_t[:, t.slot % 2, j * P:(j + 1) * P],
                                               qwin[:, t.slot, k * D:(k + 1) * D],
                                               start=False, stop=(k == 2))
                        mm.then_inc(e_pre, 1)
                    if t := at(SEG):
                        pe.wait_ge(e_lo, t.n + 1)
                        wait_from(pe, e_segs, t, 1)
                        hot = hot_slot(t)
                        for j in range(T):
                            for k in range(3):
                                mm = pe.matmul(seg_n[:, 0:D], hot[:, j * W:(j + 1) * W],
                                               h3[:, t.slot, k, j * D:(j + 1) * D],
                                               start=(j == k == 0), stop=(j == T - 1 and k == 2))
                        mm.then_inc(e_seg, 1)
                    if t := chunk_of(at(NODE)):
                        node_a(t)
                    if t := chunk_of(at(NODE + 1)):
                        node_b(t)
                pipeline(pe, NG, NODE + 1, edge_step, peeled=4)
            with pe.Else():
                with pe.Fori(0, NG) as g:
                    pe.wait_ge(g_ea, (g + 1) * 16)
                    pe.wait_ge(g_sum, g * N_SUM + 1)
                    for j in range(T):
                        mm = pe.matmul(pre[0][:, j * D:(j + 1) * D], ea[0:D1, 0, j * P:(j + 1) * P],
                                       w_ea[:, :], start=True, stop=True)
                    mm.then_inc(g_pre, 1)
                    windows(g, r[:, 1, :].rearrange("p (t f) -> p t f", t=T), D, NG, g_h, g + 1)

                def end(at):
                    node_a(at(0))
                    node_b(at(0))
                pipeline(pe, NC, 0, end, 1, peeled=2)


def kernel(x, src, dst, edge_attr_64, edge_type_16, L0_gnn_weight, L1_gnn_W1_msg, L1_gnn_b1_msg,
           L1_gnn_W2_msg, L1_gnn_b2_msg, L1_gnn_W1_upd, L1_gnn_b1_upd, L1_gnn_W2_upd, L1_gnn_b2_upd):
    import numpy as np
    import concourse.bacc as bacc
    from concourse.bass_utils import run_bass_kernel_spmd

    edges, nodes, d = src.shape[0], x.shape[0], x.shape[1]
    groups = -(-edges // GE)
    fill = groups * GE - edges

    def by_partition(a):
        a = np.asarray(a)
        a = np.concatenate([a, np.repeat(a[-1:], fill)])
        return np.ascontiguousarray(a.reshape(groups, P, T).transpose(1, 0, 2)).reshape(P, groups * T)

    def rows(a):
        return np.ascontiguousarray(a).reshape(1, -1)

    e = np.asarray(edge_attr_64)
    e = np.concatenate([e, np.repeat(e[-1:], fill, axis=0)])
    e = np.ascontiguousarray(e.reshape(groups, P, T, d).transpose(3, 0, 2, 1)).reshape(d, groups * GE)
    given = [
        ("x_t", np.ascontiguousarray(np.asarray(x).T)), ("src_tab", by_partition(src)),
        ("dst_tab", by_partition(dst)), ("type_tab", by_partition(edge_type_16)), ("edge_t", e),
        ("w_rel", np.ascontiguousarray(L0_gnn_weight)), ("w_msg1", np.ascontiguousarray(L1_gnn_W1_msg)),
        ("b_msg1", rows(L1_gnn_b1_msg)), ("w_msg2_t", np.ascontiguousarray(np.asarray(L1_gnn_W2_msg).T)),
        ("b_msg2", np.ascontiguousarray(L1_gnn_b2_msg).reshape(-1, 1)),
        ("w_upd1", np.ascontiguousarray(L1_gnn_W1_upd)), ("b_upd1", rows(L1_gnn_b1_upd)),
        ("w_upd2", np.ascontiguousarray(L1_gnn_W2_upd)), ("b_upd2", rows(L1_gnn_b2_upd)),
    ]
    nc = bacc.Bacc("TRN2", target_bir_lowering=False, num_devices=1)
    args = [nc.dram_tensor(name, a.shape, mybir.dt.from_np(a.dtype), kind="ExternalInput").ap()
            for name, a in given]
    out = nc.dram_tensor("new_x", (nodes, d), F32, kind="ExternalOutput").ap()
    gnn_kernel.edges = edges
    gnn_kernel(nc, *args, out)
    r = run_bass_kernel_spmd(nc, [dict(given)], core_ids=[0])
    return r.results[0]["new_x"]
```

```python
from collections import namedtuple
from contextlib import ExitStack

import concourse.bass as bass
from concourse import mybir

F32 = mybir.dt.float32
BF16 = mybir.dt.bfloat16
I32 = mybir.dt.int32
ALU = mybir.AluOpType
ACT = mybir.ActivationFunctionType
AX_X = mybir.AxisListType.X

P = 128
T = 8
GE = P * T
W = 128
U = 4
EPS = 1e-5
EPS_MEAN = 1e-6

Turn = namedtuple("Turn", "n round slot place")


def pipeline(eng, total, depth, step, unroll=U, peeled=1):
    ring = min(unroll, U)

    def at_constant(i):
        def at(lag):
            n = i - lag
            return Turn(n, n // ring, n % ring, n % unroll) if 0 <= n < total else None
        return at

    def at_register(k, u):
        def at(lag):
            q, place = divmod(u - lag, unroll)
            return Turn((k + q) * unroll + place, (k + q) * (unroll // ring) + place // ring,
                        place % ring, place)
        return at

    assert depth <= unroll * peeled and peeled < (total - 1) // unroll
    rounds = (total - 1) // unroll
    for i in range(peeled * unroll):
        step(at_constant(i))
    with eng.Fori(peeled, rounds) as k:
        for u in range(unroll):
            step(at_register(k, u))
    for i in range(rounds * unroll, total + depth):
        step(at_constant(i))


def chunk_of(turn):
    return Turn(turn.round, turn.round, 0, 0) if turn and turn.slot == 0 else None


def pair_of(turn):
    return Turn(turn.round * 2 + turn.slot // 2, turn.round, turn.slot // 2, 0)\
        if turn and turn.slot % 2 == 0 else None


def wait_from(eng, sem, turn, behind, unit=1):
    if isinstance(turn.n, int) and turn.n - behind + 1 <= 0:
        return
    eng.wait_ge(sem, (turn.n + (1 - behind)) * unit)


def gnn_kernel(nc, x_t, src_tab, dst_tab, type_tab, edge_t, w_rel, w_msg1, b_msg1, w_msg2_t,
               b_msg2, w_upd1, b_upd1, w_upd2, b_upd2, out):
    D, N = x_t.shape
    R = w_rel.shape[0]
    NG = src_tab.shape[1] // T
    E = 2 * edge_t.shape[1]
    assert E == NG * GE
    E_REAL = gnn_kernel.edges
    LAST = E_REAL - (NG - 1) * GE
    T_LAST = -(-LAST // P)
    assert NG % U == 0
    NB = -(-N // (2 * P)) * 2
    NP = NB * P
    NC = NB // 2
    assert NC == NG // U
    D1 = D + 1
    RD = R * D
    HALF = RD // 2
    X_FIRST = min(8 * P, N // (2 * P) * (2 * P))

    y_tab = nc.dram_tensor("y_tab", (NP * R, D), F32).ap()
    p_tab = nc.dram_tensor("p_tab", (NP, D), F32).ap()
    q_tab = nc.dram_tensor("q_tab", (NP, 3 * D), BF16).ap()

    with ExitStack() as ctx:
        def sb(name, shape, dt=F32):
            return ctx.enter_context(nc.sbuf_tensor(name, shape, dt))

        def sem(name):
            return ctx.enter_context(nc.semaphore(name))

        def sems(name, n):
            return [sem(f"{name}{i}") for i in range(n)]

        acc = sb("acc", [P, NP])
        x1u = sb("x1u", [P, NB, 2 * D])
        src_i = sb("src_i", [P, (NG + U) * T], I32)
        rel_i = sb("rel_i", [P, (NG + U) * T], I32)
        dst_i = sb("dst_i", [P, NG * T], I32)
        dloc = sb("dloc", [P, NG * T])
        spans = sb("spans", [P, 2 * NG])
        span_max = sb("span_max", [P, 2 * NG])
        done_to = sb("done_to", [P, NG])
        base_f = sb("base_f", [P, NG])
        base_i = sb("base_i", [P, NG], I32)
        fits_f = sb("fits_f", [P, 1])
        fits_i = sb("fits_i", [P, 1], I32)
        past_end = sb("past_end", [P, T])
        cur = sb("cur", [P, T])
        idx = sb("idx", [P, U, T], I32)
        gat = sb("gat", [P, U, T, D1])
        onehot = sb("onehot", [P, U, GE])
        oh_t = sb("oh_t", [P, 2, GE], BF16)
        ea = sb("ea", [P, U, GE // 2])
        qwin = sb("qwin", [P, U, 3 * D], BF16)
        r = sb("r", [P, U, T * D])
        h3 = sb("h3", [P, U, 3, T * D], BF16)
        seg_s = sb("seg_s", [P, P])
        xs = sb("xs", [D1, 2 * P])
        p_st = sb("p_st", [P, 2, D])
        q_f = sb("q_f", [P, 2, D])
        q_st = sb("q_st", [P, 2, 3, D], BF16)
        sq = sb("sq", [P, D])
        ss = sb("ss", [P, 2])
        std = sb("std", [P, 2])
        var = sb("var", [P, 2])
        step = sb("step", [P, 2])
        rstd = sb("rstd", [P, 2])
        eps = sb("eps", [P, 1])
        zero = sb("zero", [P, 1])
        deg = sb("deg", [P, 2])
        rinv = sb("rinv", [P, 2])
        pre_u = sb("pre_u", [P, 2, D])
        hu = sb("hu", [P, 2, P])
        hu_t = sb("hu_t", [D1, 2 * P])
        fin = sb("fin", [P, 2, D])
        ident = sb("ident", [P, P])
        ident_bf = sb("ident_bf", [P, P], BF16)
        iota_s = sb("iota_s", [P, W])
        center = sb("center", [D, D])
        w_parts = sb("w_parts", [P, 3, RD], BF16)
        w_ea = sb("w_ea", [P, 2 * D])
        w_raw = sb("w_raw", [D, 4 * D])
        w_mid = sb("w_mid", [D1, 4 * D])
        w_m2t = sb("w_m2t", [D, D1])
        w_u1b = sb("w_u1b", [D, D])
        w_fin = sb("w_fin", [D1, D1])
        w_u2 = sb("w_u2", [D1, D])
        w_u2c = sb("w_u2c", [D1, D])
        mean_u2 = sb("mean_u2", [D1, 1])
        bias_m = sb("bias_m", [P, D])
        bias_u = sb("bias_u", [P, D])

        y_stage = onehot
        x_rest = r[:, 0:2, :]
        x_parts = x1u[:, :, :].rearrange("p b f -> p (b f)").bitcast(BF16)
        x_hm, x_lh = x_parts[:, 0:NP], x_parts[:, NP:2 * NP]
        w_all = ea[:, :, :].rearrange("p u w -> p (u w)")
        w_y, w_rest = w_all[:, 0:RD], w_all[:, RD:2 * RD]
        w_hh, w_mm, w_hl = (w_parts[:, k, :] for k in range(3))
        hot_bf = onehot[:, :, :].rearrange("p u w -> p (u w)").bitcast(BF16)

        bank = [ctx.enter_context(nc.psum_tensor(f"bank{i}", [P, 512], F32)) for i in range(6)]
        bank_t = [ctx.enter_context(nc.psum_tensor(f"bank_t{i}", [P, GE], BF16)) for i in range(2)]
        seg = [bank[0], bank[1]]
        seg_n, seg_f = bank[0], bank[1]
        pre = [bank[2], bank[3]]
        nodes = bank[4]
        iota = bank[5]

        s_const = sem("s_const")
        s_zero = sem("s_zero")
        s_wy = sem("s_wy")
        s_w = sem("s_w")
        s_dst = sem("s_dst")
        s_tabs = sem("s_tabs")
        s_eye = sem("s_eye")
        s_iota = sem("s_iota")
        s_wps = sem("s_wps")
        s_wmid = sem("s_wmid")
        s_wfin = sem("s_wfin")
        s_whigh = sem("s_whigh")
        s_wrest = sem("s_wrest")
        s_wmiddle = sem("s_wmiddle")
        s_wlow = sem("s_wlow")
        s_sets = sem("s_sets")
        s_mean = sem("s_mean")
        s_spans = sem("s_spans")
        s_prep = sem("s_prep")
        s_base = sem("s_base")
        y_in = sems("y_in", 2)
        y_high = sem("y_high")
        y_high2 = sem("y_high2")
        y_rest = sem("y_rest")
        y_md = sem("y_md")
        y_lo = sem("y_lo")
        y_deg = sem("y_deg")
        y_mm = sem("y_mm")
        y_ev0 = sem("y_ev0")
        y_ev1 = sem("y_ev1")
        y_out = sems("y_out", U)
        pool_turns = sem("pool_turns")
        r_idx = sem("r_idx")
        r_gat = sems("r_gat", U)
        r_hot = sem("r_hot")
        r_seg = sem("r_seg")
        r_acc = sem("r_acc")
        m_x = sem("m_x")
        m_mm = sem("m_mm")
        m_ss = sem("m_ss")
        m_std = sem("m_std")
        m_rstd = sem("m_rstd")
        m_read = sem("m_read")
        m_split = sem("m_split")
        m_p = sem("m_p")
        m_pout = sem("m_pout")
        m_qout = sem("m_qout")
        m_clear = sem("m_clear")
        e_idx = sem("e_idx")
        e_gat = sems("e_gat", U)
        e_ea = sems("e_ea", U)
        e_q = sems("e_q", U)
        e_hot = sem("e_hot")
        e_tr = sem("e_tr")
        e_oht = sem("e_oht")
        e_pre = sem("e_pre")
        e_sum = sem("e_sum")
        e_hi = sem("e_hi")
        e_h = sem("e_h")
        e_rest = sem("e_rest")
        e_md = sem("e_md")
        e_lo = sem("e_lo")
        e_seg = sem("e_seg")
        e_segs = sem("e_segs")
        e_segt = sem("e_segt")
        e_acc = sem("e_acc")
        g_idx = sem("g_idx")
        g_gat = sem("g_gat")
        g_cur = sem("g_cur")
        g_hot = sem("g_hot")
        g_seg = sem("g_seg")
        g_acc = sem("g_acc")
        g_ea = sem("g_ea")
        g_pre = sem("g_pre")
        g_sum = sem("g_sum")
        g_h = sem("g_h")
        f_x = sem("f_x")
        f_mm = sem("f_mm")
        f_deg = sem("f_deg")
        f_rinv = sem("f_rinv")
        f_pre = sem("f_pre")
        f_hu = sem("f_hu")
        f_tr = sem("f_tr")
        f_hut = sem("f_hut")
        f_z = sem("f_z")
        f_ss = sem("f_ss")
        f_std = sem("f_std")
        f_rstd = sem("f_rstd")
        f_fin = sem("f_fin")
        f_out = sem("f_out")

        N_W = 12
        N_PREP = 12
        N_RSTD = 5
        N_SUM = 4
        TR, PRE, REST, SEG, ADD, NODE = 1, 2, 3, 4, 5, 11
        MIDDLE = 7
        STORE = 16
        block = ctx.enter_context(nc.Block())

        def tiles(t):
            return T_LAST if isinstance(t.n, int) and t.n == NG - 1 else T

        def gathered(t):
            return (t.round * T + tiles(t)) * 16

        def dloc_of(n):
            return dloc[:, bass.ds(n * T, T)]

        def window_onehot(eng, out_ap, d_ap):
            return eng.tensor_tensor(
                out_ap.rearrange("p (t w) -> p t w", t=T),
                iota[:, 0:W].rearrange("p (a w) -> p a w", a=1).to_broadcast([P, T, W]),
                d_ap.rearrange("p (t a) -> p t a", a=1).to_broadcast([P, T, W]), ALU.is_equal)

        def hot_slot(t):
            return hot_bf[:, t.place * GE:(t.place + 1) * GE]

        def gathered_q(j):
            return h3[:, 1, :, :].rearrange("p k f -> p (k f)")[:, j * 3 * D:(j + 1) * 3 * D]

        def by_block(ap):
            return ap.rearrange("p (b f) -> p b f", b=2)

        @block.sync
        def _(sp):
            def load_x(first, end, sem_):
                for half in range(2):
                    sp.dma_start(acc[half * D:(half + 1) * D, first:end], x_t[:, first:end])\
                        .then_inc(sem_, 16)
            load_x(0, X_FIRST, y_in[0])
            for half in range(2):
                sp.dma_start(w_y[half * D:(half + 1) * D, :].rearrange("d (r f) -> d r f", r=R),
                             w_rel.rearrange("r d f -> d r f")).then_inc(s_wy, 16)
            sp.dma_start(dst_i[:, :], dst_tab).then_inc(s_dst, 16)
            load_x(X_FIRST, N, y_in[1])
            for tab, given in ((src_i[:, 0:NG * T], src_tab), (rel_i[:, 0:NG * T], type_tab)):
                sp.dma_start(tab, given).then_inc(s_tabs, 16)
            sp.wait_ge(s_zero, 1)
            for to, of in ((w_ea[0:D, 0:D], w_msg1[0:D, :]), (w_ea[D:P, D:2 * D], w_msg1[0:D, :]),
                           (bias_m[:, :], b_msg1.to_broadcast([P, D])),
                           (w_raw[:, 0:D], w_msg1[D:2 * D, :]), (w_raw[:, D:2 * D], w_msg1[2 * D:, :]),
                           (w_raw[:, 3 * D:4 * D], w_upd1[0:D, :]), (w_u1b[:, :], w_upd1[D:, :]),
                           (w_m2t[:, 0:D], w_msg2_t), (w_m2t[:, D:D1], b_msg2),
                           (w_u2[0:D, :], w_upd2), (w_u2[D:D1, :], b_upd2),
                           (bias_u[:, :], b_upd1.to_broadcast([P, D]))):
                sp.dma_start(to, of).then_inc(s_w, 16)

            def y_step(at):
                if t := at(0):
                    sp.wait_ge(y_ev0, t.n + 1)
                    sp.wait_ge(y_ev1, t.n + 1)
                    rows = y_tab[bass.ds(t.n * (P * R), P * R), :]
                    sp.dma_start(rows.rearrange("(p r) f -> p (r f)", p=P),
                                 y_stage[:, t.slot, :]).then_inc(y_out[t.slot], 16)
            pipeline(sp, NB, 0, y_step)

            def pq_store(at):
                if t := at(0):
                    sp.wait_ge(m_p, t.n + 1)
                    sp.dma_start(
                        p_tab[bass.ds(t.n * 2 * P, 2 * P), :].rearrange("(b p) f -> p b f", p=P),
                        p_st[:, :, :]).then_inc(m_pout, 16)
                    sp.wait_ge(m_split, 4 * (t.n + 1))
                    sp.dma_start(
                        q_tab[bass.ds(t.n * 2 * P, 2 * P), :].rearrange("(b p) f -> p b f", p=P),
                        q_st[:, :, :, :].rearrange("p b k f -> p b (k f)")).then_inc(m_qout, 16)
            pipeline(sp, NC, 0, pq_store, 1)
            sp.wait_ge(m_qout, 16 * NC)

            def load_edges(sem_, slot, n):
                sp.dma_start(ea[:, slot, :], edge_t[:, bass.ds(n * (GE // 2), GE // 2)])\
                    .then_inc(sem_, 16)

            parts = -(-(N - (NC - 1) * 2 * P) // P)

            def store(t):
                sp.wait_ge(f_fin, t.n + 1)
                if isinstance(t.n, int) and t.n == NC - 1:
                    for b in range(parts):
                        first = (2 * t.n + b) * P
                        rows = min(P, N - first)
                        sp.dma_start(out[first:first + rows, :], fin[0:rows, b, :]).then_inc(f_out, 16)
                else:
                    sp.dma_start(out[bass.ds(t.n * 2 * P, 2 * P), :].rearrange("(b p) f -> p b f", p=P),
                                 fin[:, :, :]).then_inc(f_out, 16)

            fits = sp.value_load(fits_i[0:1, 0:1], min_val=0, max_val=1)
            with sp.If(fits > 0):
                def edge_step(at):
                    if t := at(0):
                        wait_from(sp, e_pre, t, U)
                        load_edges(e_ea[t.slot], t.slot, t.n)
                        base = sp.value_load(base_i[0:1, bass.ds(t.n, 1)], min_val=0, max_val=NP - W)
                        sp.dma_start(qwin[:, t.slot, :], q_tab[bass.ds(base, W), :])\
                            .then_inc(e_q[t.slot], 16)
                    if t := chunk_of(at(STORE)):
                        store(t)
                pipeline(sp, NG, STORE, edge_step, peeled=STORE // U)
            with sp.Else():
                with sp.Fori(0, NG) as g:
                    sp.wait_ge(g_pre, g + 1)
                    load_edges(g_ea, 0, g)
                pipeline(sp, NC, 0, lambda at: store(at(0)), 1)
            sp.wait_ge(f_out, 16 * (NC - 1 + parts))

        @block.gpsimd
        def _(pool):
            pool.memset(ident[:, :], 0.0).then_inc(s_const, 1)
            pool.memset(center[:, :], -1.0 / D).then_inc(s_const, 1)
            pool.memset(past_end[:, :], 1e6).then_inc(s_const, 1)
            pool.memset(eps[:, :], EPS).then_inc(s_const, 1)
            pool.iota(iota_s[:, :], [[1, W]], 0, 0, allow_small_or_imprecise_dtypes=True).then_inc(s_iota, 1)
            lim = done_to[:, :].rearrange("p (k u) -> p k u", u=U)
            pool.iota(lim, [[2 * P, NG // U], [0, U]], -2 * P, 0,
                      allow_small_or_imprecise_dtypes=True).then_inc(s_const, 1)
            pool.wait_ge(s_const, 5)
            pool.iota(lim[:, :, U - 1:U], [[2 * P, NG // U], [0, 1]], 0, 0,
                      allow_small_or_imprecise_dtypes=True).then_inc(s_const, 1)
            pool.affine_select(out=ident[:, :], in_=ident[:, :], compare_op=ALU.not_equal, fill=1.0,
                               base=0, pattern=[[-1, P]], channel_multiplier=1).then_inc(s_eye, 1)
            pool.affine_select(out=center[:, :], in_=center[:, :], compare_op=ALU.not_equal,
                               fill=1.0 - 1.0 / D, base=0, pattern=[[-1, D]],
                               channel_multiplier=1).then_inc(s_eye, 1)
            pool.affine_select(out=past_end[:, :], in_=past_end[:, :], compare_op=ALU.is_ge, fill=0.0,
                               base=-LAST, pattern=[[P, T]], channel_multiplier=1).then_inc(s_eye, 1)
            pool.wait_ge(s_eye, 3)
            pool.tensor_copy(ident_bf[:, :], ident[:, :]).then_inc(s_eye, 1)
            pool.wait_ge(s_eye, 4)
            pool.wait_ge(s_const, 6)

            pool.wait_ge(s_zero, 1)
            pool.wait_ge(y_in[0], 32)

            def y_step(at):
                if t := pair_of(at(0)):
                    if isinstance(t.n, int) and t.n * 2 * P == X_FIRST:
                        pool.wait_ge(y_in[1], 32)
                    pool.tensor_copy(x_lh[D:P, bass.ds(t.n * 2 * P, 2 * P)],
                                     acc[D:P, bass.ds(t.n * 2 * P, 2 * P)]).then_inc(y_high2, 1)
            pipeline(pool, NB, 0, y_step, peeled=3)
            pool.wait_ge(y_high2, NC)

            pool.wait_ge(s_spans, 2)
            pool.tensor_scalar(spans[:, 0:NG], spans[:, 0:NG], -1.0, None, ALU.mult).then_inc(s_prep, 1)
            pool.wait_ge(s_prep, 1)
            pool.partition_all_reduce(span_max[:, :], spans[:, :], P, bass.bass_isa.ReduceOp.max)\
                .then_inc(s_prep, 1)
            pool.wait_ge(s_prep, 2)
            pool.tensor_scalar(base_f[:, :], span_max[:, 0:NG], -1.0, float(NP - W), ALU.mult, ALU.min)\
                .then_inc(s_prep, 1)
            pool.wait_ge(s_prep, 3)
            pool.tensor_copy(base_i[:, :], base_f[:, :]).then_inc(s_prep, 1)
            pool.tensor_scalar(spans[:, 0:NG], span_max[:, NG:], 0.5 - W, None, ALU.add)\
                .then_inc(s_prep, 1)
            pool.tensor_scalar(spans[:, NG:], done_to[:, :], -0.5, None, ALU.add).then_inc(s_prep, 1)
            pool.wait_ge(s_prep, 6)
            both = spans[:, :].rearrange("p (m g) -> p m g", m=2)
            pool.tensor_tensor(both, both, base_f[:, :].rearrange("p (a g) -> p a g", a=1)
                               .to_broadcast([P, 2, NG]), ALU.subtract).then_inc(s_prep, 1)
            pool.tensor_copy(dloc[:, :], dst_i[:, :]).then_inc(s_prep, 1)
            pool.wait_ge(s_prep, 8)
            d3 = dloc[:, :].rearrange("p (g t) -> p g t", t=T)
            pool.tensor_tensor(d3, d3, base_f[:, :].rearrange("p (g a) -> p g a", a=1)
                               .to_broadcast([P, NG, T]), ALU.subtract).then_inc(s_prep, 1)
            pool.wait_ge(s_prep, 9)
            last = dloc[:, (NG - 1) * T:]
            pool.tensor_tensor(last, last, past_end[:, :], ALU.add).then_inc(s_prep, 1)
            rows_of = h3[:, :, :, :].rearrange("p u k f -> p (u k f)").bitcast(I32)[:, 0:NG * T]
            pool.wait_ge(s_tabs, 32)
            pool.tensor_scalar(rows_of, src_i[:, 0:NG * T], float(R), None, ALU.mult).then_inc(s_prep, 1)
            pool.wait_ge(s_prep, 11)
            pool.tensor_tensor(rel_i[:, 0:NG * T], rows_of, rel_i[:, 0:NG * T], ALU.add)\
                .then_inc(s_prep, 1)
            pool.wait_ge(s_base, 1)
            for s in range(U):
                pool.wait_ge(y_out[s], 16 * len(range(s, NB, U)))

            def gather(idx_sem, gat_sems, table):
                def step(at):
                    if t := at(0):
                        pool.wait_ge(idx_sem, t.n + 1)
                        pool.sem_inc(pool_turns, 1)
                        for j in range(tiles(t)):
                            pool.indirect_dma_start(
                                gat[:, t.slot, j, 0:D], None, table,
                                bass.IndirectOffsetOnAxis(ap=idx[:, t.slot, j:j + 1], axis=0)
                            ).then_inc(gat_sems[t.slot], 16)
                return step

            def gather_whole(slot, to, table):
                for j in range(T):
                    pool.indirect_dma_start(
                        to(j), None, table,
                        bass.IndirectOffsetOnAxis(ap=idx[:, slot, j:j + 1], axis=0)).then_inc(g_gat, 16)

            fits = pool.value_load(fits_i[0:1, 0:1], min_val=0, max_val=1)
            with pool.If(fits > 0):
                pipeline(pool, NG, 0, gather(r_idx, r_gat, y_tab))
            with pool.Else():
                with pool.Fori(0, NG) as g:
                    pool.wait_ge(g_idx, g + 1)
                    pool.sem_inc(pool_turns, 1)
                    gather_whole(0, lambda j: gat[:, 0, j, 0:D], y_tab)

            pool.wait_ge(m_pout, 16 * NC)
            with pool.If(fits > 0):
                pipeline(pool, NG, 0, gather(e_idx, e_gat, p_tab))
            with pool.Else():
                with pool.Fori(0, NG) as g:
                    pool.wait_ge(m_qout, 16 * NC)
                    pool.wait_ge(g_idx, NG + g + 1)
                    pool.sem_inc(pool_turns, 1)
                    gather_whole(0, lambda j: gat[:, 0, j, 0:D], p_tab)
                    gather_whole(1, gathered_q, q_tab)

        @block.scalar
        def _(act):
            act.wait_ge(s_iota, 1)
            act.activation(iota[:, 0:W], iota_s[:, :], ACT.Copy).then_inc(s_iota, 1)
            act.wait_ge(s_zero, 1)
            act.wait_ge(s_wy, 32)
            act.activation(w_hh, w_y, ACT.Copy).then_inc(s_whigh, 1)
            act.activation(w_hl[0:D, :], w_y[0:D, :], ACT.Copy)
            act.wait_ge(y_in[0], 32)

            def y_step(at):
                if t := pair_of(at(0)):
                    if isinstance(t.n, int) and t.n * 2 * P == X_FIRST:
                        act.wait_ge(y_in[1], 32)
                    cols = bass.ds(t.n * 2 * P, 2 * P)
                    act.activation(x_hm[0:D, cols], acc[0:D, cols], ACT.Copy).then_inc(y_high, 1)
                    if isinstance(t.n, int) and t.n == 0:
                        act.wait_ge(s_wrest, 1)
                        act.activation(w_mm, w_rest, ACT.Copy).then_inc(s_wmiddle, 1)
                if t := pair_of(at(2)):
                    cols = bass.ds(t.n * 2 * P, 2 * P)
                    act.wait_ge(y_rest, 2 * (t.n + 1))
                    act.activation(x_lh[0:D, cols], x_rest[0:D, t.slot, 0:2 * P], ACT.Copy)\
                        .then_inc(y_md, 1)
                    act.activation(x_hm[D:P, cols], x_rest[D:P, t.slot, 0:2 * P], ACT.Copy)\
                        .then_inc(y_md, 1)
                    act.activation(acc[D:D1, cols], zero[D:D1, :].to_broadcast([1, 2 * P]), ACT.Copy)\
                        .then_inc(y_deg, 1)
                if t := at(5):
                    act.wait_ge(y_mm, t.n + 1)
                    if not (isinstance(t.n, int) and t.n < U):
                        act.wait_ge(y_out[t.slot], t.round * 16)
                    act.activation(y_stage[:, t.slot, 0:HALF], bank[2 * (t.slot % 2)][:, 0:HALF],
                                   ACT.Copy).then_inc(y_ev0, 1)
            pipeline(act, NB, 5, y_step, peeled=3)

            def stage_x(t, sem_, used):
                wait_from(act, used, t, 1)
                act.activation(xs[:, :], acc[0:D1, bass.ds(t.n * 2 * P, 2 * P)], ACT.Copy)\
                    .then_inc(sem_, 1)

            def deviation(t, first, stride, ready, ss_sem, std_sem, used):
                act.wait_ge(ready, t.n + 1)
                for b in range(2):
                    if b or not isinstance(t.n, int) or t.n:
                        act.wait_ge(ss_sem, t.n * 2 + b)
                    act.activation(sq[:, :], nodes[:, first + b * stride:first + b * stride + D],
                                   ACT.Square, accum_out=ss[:, b:b + 1]).then_inc(ss_sem, 1)
                act.wait_ge(ss_sem, (t.n + 1) * 2)
                wait_from(act, used, t, 1, N_RSTD)
                act.activation(std[:, :], ss[:, :], ACT.Sqrt, bias=eps[:, 0:1], scale=1.0 / D)\
                    .then_inc(std_sem, 1)

            act.wait_ge(s_base, 1)
            act.wait_ge(s_const, 6)

            def middle(at):
                if t := at(0):
                    act.wait_ge(r_acc, min(U * t.n + U + 3, NG) if isinstance(t.n, int)
                                else t.n * U + (U + 3))
                    stage_x(t, m_x, m_mm)
                    deviation(t, 2 * D, 4 * D, m_mm, m_ss, m_std, m_rstd)
            pipeline(act, NC, 0, middle, 1, peeled=2)

            def node_a(t):
                stage_x(t, f_x, f_mm)

            def node_b(t):
                act.wait_ge(f_pre, 2 * (t.n + 1))
                wait_from(act, f_tr, t, 1)
                act.activation(hu[:, :, 0:D], pre_u[:, :, :], ACT.Silu).then_inc(f_hu, 1)
                act.wait_ge(f_tr, t.n + 1)
                wait_from(act, f_z, t, 1)
                act.activation(hu_t[:, :], nodes[0:D1, 0:2 * P], ACT.Copy).then_inc(f_hut, 1)
                deviation(t, 2 * P, D, f_z, f_ss, f_std, f_rstd)

            fits = act.value_load(fits_i[0:1, 0:1], min_val=0, max_val=1)
            with act.If(fits > 0):
                def edge_step(at):
                    if t := at(TR):
                        act.wait_ge(e_tr, t.n + 1)
                        wait_from(act, e_pre, t, 2)
                        n = tiles(t) * P
                        act.activation(oh_t[:, t.slot % 2, 0:n], bank_t[t.slot % 2][:, 0:n], ACT.Copy)\
                            .then_inc(e_oht, 1)
                    if t := at(REST):
                        act.wait_ge(e_rest, t.n + 1)
                        n = tiles(t) * D
                        act.activation(h3[:, t.slot, 1, 0:n], r[:, t.slot, 0:n], ACT.Copy)\
                            .then_inc(e_md, 1)
                    if t := at(PRE):
                        act.wait_ge(e_sum, t.n + 1)
                        wait_from(act, e_seg, t, U)
                        n = tiles(t) * D
                        act.activation(h3[:, t.slot, 0, 0:n], r[:, t.slot, 0:n], ACT.Silu)\
                            .then_inc(e_hi, 1)
                        act.activation(r[:, t.slot, 0:n], r[:, t.slot, 0:n], ACT.Silu).then_inc(e_h, 1)
                    if t := at(SEG):
                        act.wait_ge(e_seg, t.n + 1)
                        wait_from(act, e_segt, t, 1)
                        act.activation(seg_s[:, 0:D], seg_n[:, 0:D], ACT.Copy).then_inc(e_segs, 1)
                    if t := chunk_of(at(NODE)):
                        act.wait_ge(e_acc, min(U * t.n + U + 3, NG) if isinstance(t.n, int)
                                    else t.n * U + (U + 3))
                        node_a(t)
                    if t := chunk_of(at(NODE + 1)):
                        node_b(t)
                pipeline(act, NG, NODE + 1, edge_step, unroll=2 * U, peeled=2)
            with act.Else():
                with act.Fori(0, NG) as g:
                    act.wait_ge(g_sum, g * N_SUM + N_SUM + 1)
                    act.wait_ge(g_acc, (g + NG) * NB + 1)
                    act.activation(r[:, 1, :], r[:, 0, :], ACT.Silu).then_inc(g_h, 1)
                act.wait_ge(g_acc, 1 + 2 * NG * NB)

                def end(at):
                    node_a(at(0))
                    node_b(at(0))
                pipeline(act, NC, 0, end, 1)

        @block.vector
        def _(dve):
            dve.memset(src_i[:, NG * T:], 0)
            dve.memset(rel_i[:, NG * T:], 0)
            dve.memset(w_mid[D:D1, :], 0)
            dve.memset(w_fin[:, D:D1], 0)
            dve.memset(hu[:, :, :], 0)
            dve.memset(seg_s[:, :], 0)
            dve.memset(zero[:, :], 0)
            dve.memset(w_ea[:, :], 0)
            dve.memset(acc[:, N:NP], 0)
            dve.memset(gat[:, :, :, D:D1], 1.0).then_inc(s_sets, 1)
            dve.wait_ge(s_sets, 1)
            dve.memset(w_fin[D:D1, D:D1], 1.0)
            dve.memset(hu[:, :, D:D1], 1.0).then_inc(s_zero, 1)
            dve.wait_ge(s_whigh, 1)
            dve.tensor_tensor(w_rest, w_y, w_hh, ALU.subtract).then_inc(s_wrest, 1)

            d3 = dst_i[:, :].rearrange("p (g t) -> p g t", t=T)

            def center_weights():
                dve.wait_ge(s_w, 16 * N_W)
                dve.tensor_reduce(mean_u2[:, :], w_u2[:, :], AX_X, ALU.add).then_inc(s_mean, 1)
                dve.wait_ge(s_eye, 2)
                dve.tensor_copy(w_raw[:, 2 * D:3 * D], ident[0:D, 0:D]).then_inc(s_wmid, 1)
                dve.wait_ge(s_mean, 1)
                dve.tensor_scalar(mean_u2[:, :], mean_u2[:, :], -1.0 / D, None, ALU.mult)\
                    .then_inc(s_mean, 1)
                dve.wait_ge(s_mean, 2)
                dve.tensor_scalar(w_u2c[:, :], w_u2[:, :], mean_u2[:, 0:1], None, ALU.add)\
                    .then_inc(s_wfin, 1)

            def decide():
                dve.wait_ge(s_prep, N_PREP)
                dve.tensor_reduce(fits_f[:, :], spans[:, :], AX_X, ALU.max).then_inc(s_mean, 1)
                dve.wait_ge(s_mean, 3)
                dve.tensor_scalar(fits_i[:, :], fits_f[:, :], 0.0, None, ALU.is_lt).then_inc(s_base, 1)

            def y_step(at):
                if t := pair_of(at(0)):
                    cols = bass.ds(t.n * 2 * P, 2 * P)
                    dve.wait_ge(y_high, t.n + 1)
                    wait_from(dve, y_md, t, 2, 2)
                    wait_from(dve, y_lo, t, 2)
                    dve.tensor_tensor(x_rest[0:D, t.slot, 0:2 * P], acc[0:D, cols], x_hm[0:D, cols],
                                      ALU.subtract).then_inc(y_rest, 1)
                    dve.wait_ge(y_high2, t.n + 1)
                    dve.tensor_tensor(x_rest[D:P, t.slot, 0:2 * P], acc[D:P, cols], x_lh[D:P, cols],
                                      ALU.subtract).then_inc(y_rest, 1)
                    if isinstance(t.n, int) and t.n == 0:
                        dve.wait_ge(s_wmiddle, 1)
                        dve.tensor_tensor(w_hl[D:P, :], w_rest[D:P, :], w_mm[D:P, :], ALU.subtract)\
                            .then_inc(s_wlow, 1)
                if t := pair_of(at(2)):
                    cols = bass.ds(t.n * 2 * P, 2 * P)
                    dve.wait_ge(y_md, 2 * (t.n + 1))
                    dve.tensor_tensor(x_lh[0:D, cols], x_rest[0:D, t.slot, 0:2 * P], x_lh[0:D, cols],
                                      ALU.subtract).then_inc(y_lo, 1)
                if t := at(5):
                    dve.wait_ge(y_mm, t.n + 1)
                    if not (isinstance(t.n, int) and t.n < U):
                        dve.wait_ge(y_out[t.slot], t.round * 16)
                    dve.tensor_copy(y_stage[:, t.slot, HALF:RD], bank[2 * (t.slot % 2) + 1][:, 0:HALF])\
                        .then_inc(y_ev1, 1)
                    if isinstance(t.n, int) and t.n == 1:
                        dve.wait_ge(s_dst, 16)
                        dve.tensor_reduce(spans[:, 0:NG], d3, AX_X, ALU.min).then_inc(s_spans, 1)
                    if isinstance(t.n, int) and t.n == 2:
                        dve.tensor_reduce(spans[:, NG:], d3, AX_X, ALU.max).then_inc(s_spans, 1)
                    if isinstance(t.n, int) and t.n == NB - 5:
                        center_weights()
                    if isinstance(t.n, int) and t.n == NB - 3:
                        decide()
            pipeline(dve, NB, 5, y_step, peeled=3)

            dve.wait_ge(s_wps, 2)
            dve.tensor_copy(w_mid[0:D, :], nodes[0:D, 0:4 * D]).then_inc(s_wmid, 1)
            dve.tensor_copy(w_fin[:, 0:D], nodes[0:D1, 4 * D:5 * D]).then_inc(s_wfin, 1)
            dve.wait_ge(s_base, 1)
            dve.wait_ge(s_iota, 2)
            dve.wait_ge(y_deg, NC)
            for s in range(U):
                dve.wait_ge(y_out[s], 16 * len(range(s, NB, U)))

            fits = dve.value_load(fits_i[0:1, 0:1], min_val=0, max_val=1)

            def put_idx(n, slot, table, sem_):
                dve.tensor_copy(idx[:, slot, :], table[:, bass.ds(n * T, T)]).then_inc(sem_, 1)

            def add_window(t, ps, rows, sem_):
                base = dve.value_load(base_i[0:1, bass.ds(t.n, 1)], min_val=0, max_val=NP - W)
                wait_from(dve, sem_, t, 1)
                win = acc[0:rows, bass.ds(base, W)]
                dve.tensor_tensor(win, ps[0:rows, 0:W], win, ALU.add).then_inc(sem_, 1)

            def windows(g, rows, first):
                dve.tensor_scalar(cur[:, :], dloc_of(g), base_f[:, bass.ds(g, 1)], None, ALU.add)\
                    .then_inc(g_cur, 1)
                with dve.Fori(0, NB) as w:
                    done = (g + first) * NB + w
                    dve.wait_ge(g_cur, done + (g + first) + 1)
                    window_onehot(dve, onehot[:, 0, :], cur[:, :]).then_inc(g_hot, 1)
                    dve.wait_ge(g_hot, done + 1)
                    dve.tensor_scalar(cur[:, :], cur[:, :], -float(W), None, ALU.add)\
                        .then_inc(g_cur, 1)
                    dve.wait_ge(g_seg, done + 1)
                    win = acc[0:rows, bass.ds(w * W, W)]
                    dve.tensor_tensor(win, seg[0][0:rows, 0:W], win, ALU.add).then_inc(g_acc, 1)
                    dve.wait_ge(g_acc, done + 2)

            def over_features(ap):
                return ap.rearrange("p (b a) -> p b a", a=1).to_broadcast([P, 2, D])

            def inverse_deviation(t, std_sem, sem_, used):
                dve.wait_ge(std_sem, t.n + 1)
                wait_from(dve, used, t, 1)
                dve.tensor_scalar(var[:, :], ss[:, :], 1.0 / D, EPS, ALU.mult, ALU.add).then_inc(sem_, 1)
                dve.reciprocal(rstd[:, :], std[:, :]).then_inc(sem_, 1)
                dve.wait_ge(sem_, t.n * N_RSTD + 2)
                dve.scalar_tensor_tensor(step[:, :], rstd[:, :], -0.5, rstd[:, :], ALU.mult, ALU.mult)\
                    .then_inc(sem_, 1)
                dve.wait_ge(sem_, t.n * N_RSTD + 3)
                dve.tensor_tensor(step[:, :], step[:, :], var[:, :], ALU.mult).then_inc(sem_, 1)
                dve.wait_ge(sem_, t.n * N_RSTD + 4)
                dve.scalar_tensor_tensor(rstd[:, :], step[:, :], 1.5, rstd[:, :], ALU.add, ALU.mult)\
                    .then_inc(sem_, 1)
                dve.wait_ge(sem_, t.n * N_RSTD + N_RSTD)

            def middle(t):
                inverse_deviation(t, m_std, m_rstd, m_read)
                if not (isinstance(t.n, int) and t.n == 0):
                    dve.wait_ge(m_pout, t.n * 16)
                ps = by_block(nodes[:, :])
                scale = over_features(rstd[:, :])
                x1 = x1u[:, bass.ds(t.n * 2, 2), 0:D]
                dve.tensor_tensor(p_st[:, :, :], ps[:, :, 0:D], scale, ALU.mult).then_inc(m_p, 1)
                for b in range(2):
                    ins = dve.scalar_tensor_tensor(q_f[:, b, :], ps[:, b, D:2 * D], rstd[:, b:b + 1],
                                                   bias_m[:, :], ALU.mult, ALU.add)
                ins.then_inc(m_split, 1)
                dve.tensor_tensor(x1, ps[:, :, 2 * D:3 * D], scale, ALU.mult)
                for b in range(2):
                    u = x1u[:, bass.ds(t.n * 2 + b, 1), D:2 * D].rearrange("p a f -> p (a f)")
                    ins = dve.scalar_tensor_tensor(u, ps[:, b, 3 * D:4 * D], rstd[:, b:b + 1],
                                                   bias_u[:, :], ALU.mult, ALU.add)
                ins.then_inc(m_read, 1)

            def split(t):
                if not (isinstance(t.n, int) and t.n == 0):
                    dve.wait_ge(m_qout, t.n * 16)
                dve.wait_ge(m_split, t.n * 4 + 1)
                dve.tensor_copy(q_st[:, :, 0, :], q_f[:, :, :]).then_inc(m_split, 1)
                dve.wait_ge(m_split, t.n * 4 + 2)
                dve.tensor_tensor(q_f[:, :, :], q_f[:, :, :], q_st[:, :, 0, :], ALU.subtract)\
                    .then_inc(m_clear, 1)
                dve.wait_ge(m_clear, t.n * 2 + 1)
                dve.tensor_copy(q_st[:, :, 1, :], q_f[:, :, :]).then_inc(m_split, 1)
                dve.tensor_copy(acc[0:D, bass.ds(t.n * 2 * P, 2 * P)],
                                zero[0:D, :].to_broadcast([D, 2 * P])).then_inc(m_clear, 1)
                dve.wait_ge(m_split, t.n * 4 + 3)
                dve.tensor_tensor(q_st[:, :, 2, :], q_f[:, :, :], q_st[:, :, 1, :], ALU.subtract)\
                    .then_inc(m_split, 1)

            with dve.If(fits > 0):
                for s in range(U):
                    put_idx(s, s, rel_i, r_idx)

                def rel_step(at):
                    if t := at(0):
                        wait_from(dve, r_seg, t, U)
                        window_onehot(dve, onehot[:, t.slot, :], dloc_of(t.n)).then_inc(r_hot, 1)
                    if t := at(1):
                        dve.wait_ge(r_seg, t.n + 1)
                        put_idx(t.n + U, t.slot, rel_i, r_idx)
                        add_window(t, seg[t.slot % 2], D1, r_acc)
                    if t := chunk_of(at(MIDDLE)):
                        middle(t)
                    if t := chunk_of(at(MIDDLE + 1)):
                        split(t)
                pipeline(dve, NG, MIDDLE + 1, rel_step, peeled=3)
            with dve.Else():
                dve.sem_inc(g_acc, 1)
                dve.sem_inc(g_sum, 1)
                with dve.Fori(0, NG) as g:
                    put_idx(g, 0, rel_i, g_idx)
                    windows(g, D1, 0)
                dve.sem_inc(r_acc, NG)

                def between(at):
                    middle(at(0))
                    split(at(0))
                pipeline(dve, NC, 0, between, 1, peeled=2)
            dve.wait_ge(m_clear, 2 * NC)

            def node_a(t):
                dve.wait_ge(f_mm, t.n + 1)
                ps = by_block(nodes[:, 0:2 * D1])
                dve.tensor_scalar(deg[:, :], ps[:, :, D], EPS_MEAN, None, ALU.add).then_inc(f_deg, 1)
                dve.wait_ge(f_deg, t.n + 1)
                wait_from(dve, f_pre, t, 1, 2)
                dve.reciprocal(rinv[:, :], deg[:, :]).then_inc(f_rinv, 1)
                dve.wait_ge(f_rinv, t.n + 1)
                wait_from(dve, f_hu, t, 1)
                for b in range(2):
                    u = x1u[:, bass.ds(t.n * 2 + b, 1), D:2 * D].rearrange("p a f -> p (a f)")
                    dve.scalar_tensor_tensor(pre_u[:, b, :], ps[:, b, 0:D], rinv[:, b:b + 1], u,
                                             ALU.mult, ALU.add).then_inc(f_pre, 1)

            def node_c(t):
                inverse_deviation(t, f_std, f_rstd, f_fin)
                if not (isinstance(t.n, int) and t.n == 0):
                    dve.wait_ge(f_out, t.n * 16)
                dve.tensor_tensor(fin[:, :, :], by_block(nodes[:, 2 * P:2 * P + 2 * D]),
                                  over_features(rstd[:, :]), ALU.mult).then_inc(f_fin, 1)

            with dve.If(fits > 0):
                for s in range(U):
                    put_idx(s, s, src_i, e_idx)

                def edge_step(at):
                    if t := at(0):
                        wait_from(dve, e_seg, t, 2 * U)
                        window_onehot(dve, hot_slot(t), dloc_of(t.n)).then_inc(e_hot, 1)
                    if t := at(SEG):
                        dve.wait_ge(e_md, t.n + 1)
                        n = tiles(t) * D
                        dve.tensor_tensor(h3[:, t.slot, 2, 0:n], r[:, t.slot, 0:n], h3[:, t.slot, 1, 0:n],
                                          ALU.subtract).then_inc(e_lo, 1)
                    if t := at(REST):
                        dve.wait_ge(e_h, t.n + 1)
                        n = tiles(t) * D
                        dve.tensor_tensor(r[:, t.slot, 0:n], r[:, t.slot, 0:n], h3[:, t.slot, 0, 0:n],
                                          ALU.subtract).then_inc(e_rest, 1)
                    if t := at(ADD):
                        dve.wait_ge(e_segt, t.n + 1)
                        add_window(t, seg_f, D, e_acc)
                    if t := at(PRE):
                        dve.wait_ge(e_pre, t.n + 1)
                        dve.wait_ge(e_gat[t.slot], gathered(t))
                        wait_from(dve, e_lo, t, U)
                        n = tiles(t)
                        dve.tensor_tensor(r[:, t.slot, 0:n * D].rearrange("p (t f) -> p t f", t=n),
                                          pre[t.slot % 2][:, 0:n * D].rearrange("p (t f) -> p t f", t=n),
                                          gat[:, t.slot, 0:n, 0:D], ALU.add).then_inc(e_sum, 1)
                        dve.wait_ge(e_sum, t.n + 1)
                        put_idx(t.n + U, t.slot, src_i, e_idx)
                    if t := chunk_of(at(NODE)):
                        node_a(t)
                    if t := chunk_of(at(NODE + 2)):
                        node_c(t)
                pipeline(dve, NG, NODE + 2, edge_step, unroll=2 * U, peeled=2)
            with dve.Else():
                with dve.Fori(0, NG) as g:
                    dve.tensor_copy(idx[:, 1, :], dst_i[:, bass.ds(g * T, T)])
                    put_idx(g, 0, src_i, g_idx)
                    dve.wait_ge(g_pre, g + 2)
                    dve.wait_ge(g_gat, g * (32 * T) + (NG * 16 * T + 32 * T))
                    to = r[:, 0, :].rearrange("p (t f) -> p t f", t=T)
                    q3 = h3[:, 1, :, :].rearrange("p k f -> p (k f)").rearrange(
                        "p (t k f) -> p t k f", t=T, k=3)
                    before = pre[0][:, :].rearrange("p (t f) -> p t f", t=T)
                    for k, more in enumerate((gat[:, 0, :, 0:D], q3[:, :, 0, :], q3[:, :, 1, :],
                                              q3[:, :, 2, :])):
                        if k:
                            dve.wait_ge(g_sum, g * N_SUM + (k + 1))
                        dve.tensor_tensor(to, before, more, ALU.add).then_inc(g_sum, 1)
                        before = to
                    windows(g, D, NG)

                def end(at):
                    node_a(at(0))
                    node_c(at(0))
                pipeline(dve, NC, 0, end, 1, peeled=2)

        @block.tensor
        def _(pe):
            pe.wait_ge(s_wlow, 1)

            def y_step(at):
                if t := at(4):
                    if pair := pair_of(t):
                        pe.wait_ge(y_lo, pair.n + 1)
                    wait_from(pe, y_ev0, t, 2)
                    wait_from(pe, y_ev1, t, 2)
                    for half in range(2):
                        o = bank[2 * (t.slot % 2) + half][:, 0:HALF]
                        cols = slice(half * HALF, (half + 1) * HALF)
                        parts = ((x_hm, w_hh), (x_hm, w_mm), (x_lh, w_hl))
                        for k, (xp, wp) in enumerate(parts):
                            mm = pe.matmul(o, xp[:, bass.ds(t.n * P, P)], wp[:, cols], start=(k == 0),
                                           stop=(k == len(parts) - 1))
                    mm.then_inc(y_mm, 1)
            pipeline(pe, NB, 4, y_step, peeled=2)

            pe.wait_ge(s_w, 16 * N_W)
            pe.wait_ge(s_eye, 4)
            pe.wait_ge(s_wmid, 1)
            pe.wait_ge(s_zero, 1)
            pe.matmul(nodes[0:D, 0:4 * D], center[:, :], w_raw[:, :], start=True, stop=True)\
                .then_inc(s_wps, 1)
            pe.matmul(nodes[0:D1, 4 * D:5 * D], w_m2t[:, :], w_u1b[:, :], start=True, stop=True)\
                .then_inc(s_wps, 1)

            def segment_sums(ps, rows, width, hot, n=T):
                for j in range(n):
                    mm = pe.matmul(ps[0:width, 0:W], rows[:, j, :], hot[:, j * W:(j + 1) * W],
                                   start=(j == 0), stop=(j == n - 1))
                return mm

            def windows(g, rows, width, first, rows_sem, rows_there):
                with pe.Fori(0, NB) as w:
                    done = (g + first) * NB + w
                    pe.wait_ge(rows_sem, rows_there)
                    pe.wait_ge(g_hot, done + 1)
                    pe.wait_ge(g_acc, done + 1)
                    segment_sums(seg[0], rows, width, onehot[:, 0, :]).then_inc(g_seg, 1)

            def middle(t):
                pe.wait_ge(m_x, t.n + 1)
                wait_from(pe, m_read, t, 1)
                for b in range(2):
                    mm = pe.matmul(nodes[:, b * 4 * D:(b + 1) * 4 * D], xs[:, b * P:(b + 1) * P],
                                   w_mid[:, :], start=True, stop=True)
                mm.then_inc(m_mm, 1)

            pe.wait_ge(s_base, 1)
            pe.wait_ge(s_wmid, 2)
            pe.wait_ge(s_wfin, 2)
            fits = pe.value_load(fits_i[0:1, 0:1], min_val=0, max_val=1)
            with pe.If(fits > 0):
                def rel_step(at):
                    if t := chunk_of(at(MIDDLE)):
                        middle(t)
                    if t := at(0):
                        pe.wait_ge(r_hot, t.n + 1)
                        pe.wait_ge(r_gat[t.slot], gathered(t))
                        wait_from(pe, r_acc, t, 2)
                        segment_sums(seg[t.slot % 2], gat[:, t.slot, :, :], D1, onehot[:, t.slot, :],
                                     tiles(t))\
                            .then_inc(r_seg, 1)
                pipeline(pe, NG, MIDDLE, rel_step, peeled=3)
            with pe.Else():
                pe.sem_inc(g_pre, 1)
                with pe.Fori(0, NG) as g:
                    windows(g, gat[:, 0, :, :], D1, 0, g_gat, (g + 1) * (16 * T))
                pipeline(pe, NC, 0, lambda at: middle(at(0)), 1, peeled=2)
            pe.wait_ge(m_read, NC)

            def node_a(t):
                pe.wait_ge(f_x, t.n + 1)
                wait_from(pe, f_fin, t, 1)
                for b in range(2):
                    mm = pe.matmul(nodes[:, b * D1:(b + 1) * D1], xs[:, b * P:(b + 1) * P],
                                   w_fin[:, :], start=True, stop=True)
                mm.then_inc(f_mm, 1)

            def node_b(t):
                pe.wait_ge(f_hu, t.n + 1)
                for b in range(2):
                    mm = pe.transpose(nodes[:, b * P:(b + 1) * P], hu[:, b, :], ident[:, :])
                mm.then_inc(f_tr, 1)
                pe.wait_ge(f_hut, t.n + 1)
                for b in range(2):
                    o = nodes[:, 2 * P + b * D:2 * P + (b + 1) * D]
                    pe.matmul(o, hu_t[:, b * P:(b + 1) * P], w_u2c[:, :], start=True, stop=False)
                    x1 = x1u[:, bass.ds(t.n * 2 + b, 1), 0:D].rearrange("p a f -> p (a f)")
                    mm = pe.matmul(o, ident[:, :], x1, start=False, stop=True)
                mm.then_inc(f_z, 1)

            def edge_products(ps, slot, stop, n=T):
                for j in range(0, n, 2):
                    mm = pe.matmul(ps[:, j * D:(j + 2) * D], ea[:, slot, j // 2 * P:(j // 2 + 1) * P],
                                   w_ea[:, :], start=(j == 0), stop=stop and j == T - 2)
                return mm

            with pe.If(fits > 0):
                def edge_step(at):
                    if t := at(TR):
                        pe.wait_ge(e_hot, t.n + 1)
                        wait_from(pe, e_oht, t, 2)
                        hot = hot_slot(t)
                        for j in range(tiles(t)):
                            mm = pe.transpose(bank_t[t.slot % 2][:, j * P:(j + 1) * P],
                                              hot[:, j * W:(j + 1) * W], ident_bf[:, :])
                        mm.then_inc(e_tr, 1)
                    if t := at(ADD):
                        pe.wait_ge(e_segs, t.n + 1)
                        wait_from(pe, e_acc, t, 1)
                        pe.transpose(seg_f[:, 0:P], seg_s[:, :], ident[:, :]).then_inc(e_segt, 1)
                    if t := at(PRE):
                        pe.wait_ge(e_oht, t.n + 1)
                        pe.wait_ge(e_ea[t.slot], (t.round + 1) * 16)
                        pe.wait_ge(e_q[t.slot], (t.round + 1) * 16)
                        wait_from(pe, e_sum, t, 2)
                        edge_products(pre[t.slot % 2], t.slot, False, tiles(t))
                        for j in range(tiles(t)):
                            o = pre[t.slot % 2][:, j * D:(j + 1) * D]
                            for k in range(3):
                                mm = pe.matmul(o, oh_t[:, t.slot % 2, j * P:(j + 1) * P],
                                               qwin[:, t.slot, k * D:(k + 1) * D],
                                               start=False, stop=(j == tiles(t) - 1 and k == 2))
                        mm.then_inc(e_pre, 1)
                    if t := at(SEG):
                        pe.wait_ge(e_lo, t.n + 1)
                        wait_from(pe, e_segs, t, 1)
                        hot = hot_slot(t)
                        n = tiles(t)
                        for j in range(n):
                            for k in range(3):
                                mm = pe.matmul(seg_n[:, 0:D], hot[:, j * W:(j + 1) * W],
                                               h3[:, t.slot, k, j * D:(j + 1) * D],
                                               start=(j == k == 0), stop=(j == n - 1 and k == 2))
                        mm.then_inc(e_seg, 1)
                    if t := chunk_of(at(NODE)):
                        node_a(t)
                    if t := chunk_of(at(NODE + 1)):
                        node_b(t)
                pipeline(pe, NG, NODE + 1, edge_step, unroll=2 * U, peeled=2)
            with pe.Else():
                with pe.Fori(0, NG) as g:
                    pe.wait_ge(g_ea, (g + 1) * 16)
                    pe.wait_ge(g_sum, g * N_SUM + 1)
                    edge_products(pre[0], 0, True).then_inc(g_pre, 1)
                    windows(g, r[:, 1, :].rearrange("p (t f) -> p t f", t=T), D, NG, g_h, g + 1)

                def end(at):
                    node_a(at(0))
                    node_b(at(0))
                pipeline(pe, NC, 0, end, 1, peeled=2)


def kernel(x, src, dst, edge_attr_64, edge_type_16, L0_gnn_weight, L1_gnn_W1_msg, L1_gnn_b1_msg,
           L1_gnn_W2_msg, L1_gnn_b2_msg, L1_gnn_W1_upd, L1_gnn_b1_upd, L1_gnn_W2_upd, L1_gnn_b2_upd):
    import numpy as np
    import concourse.bacc as bacc
    from concourse.bass_utils import run_bass_kernel_spmd

    edges, nodes, d = src.shape[0], x.shape[0], x.shape[1]
    groups = -(-edges // GE)
    fill = groups * GE - edges

    def by_group(a):
        a = np.asarray(a)
        a = np.concatenate([a, np.repeat(a[-1:], fill, axis=0)])
        tail = a[-GE:].reshape(1, T, P, *a.shape[1:]).swapaxes(1, 2)
        return np.concatenate([a[:-GE].reshape(groups - 1, P, T, *a.shape[1:]), tail])

    def by_partition(a):
        return np.ascontiguousarray(by_group(a).transpose(1, 0, 2)).reshape(P, groups * T)

    def rows(a):
        return np.ascontiguousarray(a).reshape(1, -1)

    e = by_group(edge_attr_64).reshape(groups, P, T // 2, 2, d).transpose(3, 4, 0, 2, 1)
    e = np.ascontiguousarray(e).reshape(2 * d, groups * GE // 2)
    given = [
        ("x_t", np.ascontiguousarray(np.asarray(x).T)), ("src_tab", by_partition(src)),
        ("dst_tab", by_partition(dst)), ("type_tab", by_partition(edge_type_16)), ("edge_t", e),
        ("w_rel", np.ascontiguousarray(L0_gnn_weight)), ("w_msg1", np.ascontiguousarray(L1_gnn_W1_msg)),
        ("b_msg1", rows(L1_gnn_b1_msg)), ("w_msg2_t", np.ascontiguousarray(np.asarray(L1_gnn_W2_msg).T)),
        ("b_msg2", np.ascontiguousarray(L1_gnn_b2_msg).reshape(-1, 1)),
        ("w_upd1", np.ascontiguousarray(L1_gnn_W1_upd)), ("b_upd1", rows(L1_gnn_b1_upd)),
        ("w_upd2", np.ascontiguousarray(L1_gnn_W2_upd)), ("b_upd2", rows(L1_gnn_b2_upd)),
    ]
    nc = bacc.Bacc("TRN2", target_bir_lowering=False, num_devices=1)
    args = [nc.dram_tensor(name, a.shape, mybir.dt.from_np(a.dtype), kind="ExternalInput").ap()
            for name, a in given]
    out = nc.dram_tensor("new_x", (nodes, d), F32, kind="ExternalOutput").ap()
    gnn_kernel.edges = edges
    gnn_kernel(nc, *args, out)
    r = run_bass_kernel_spmd(nc, [dict(given)], core_ids=[0])
    return r.results[0]["new_x"]
```
